# Optimizing a Trainium2 kernel written in Bass

```python
import numpy as np
import jax
import jax.numpy as jnp

def _softmax(x, axis=-1):
    return jax.nn.softmax(x, axis=axis)

def _gelu(x):
    return jax.nn.gelu(x, approximate=True)

def _silu(x):
    return jax.nn.silu(x)

def _sigmoid(x):
    return jax.nn.sigmoid(x)

def _layernorm(x, axis=-1, eps=1e-05):
    m = jnp.mean(x, axis=axis, keepdims=True)
    v = jnp.var(x, axis=axis, keepdims=True)
    return (x - m) / jnp.sqrt(v + eps)

def _scatter_add(tgt, idx, src, axis=0):
    return tgt.at[idx].add(src)

def _segment_sum(src, seg, n):
    return jax.ops.segment_sum(src, seg, n)
kernel_name = 'mk_seq_preln_d1_jaxref_r8_7dd5a8'

def setup_inputs(seed: int=0):
    np.random.seed(seed)
    _w = jnp.asarray

    def _L0_attn_setup():
        import jax, jax.numpy as jnp
        import numpy as np
        LN_EPS = 1e-05
        key = jax.random.key(seed)
        ks = jax.random.split(key, 4)
        B_, S, D = (32, 128, 128)
        return {'x': jax.random.normal(ks[0], (B_, S, D), dtype=jnp.float32), 'A': jax.random.normal(ks[1], (D, D), dtype=jnp.float32) * 0.01, 'B': jax.random.normal(ks[2], (D, D), dtype=jnp.float32) * 0.01, 'C': jax.random.normal(ks[3], (D, D), dtype=jnp.float32) * 0.01, 'gamma': jnp.ones((D,), dtype=jnp.float32), 'beta': jnp.zeros((D,), dtype=jnp.float32)}
    _L0_attn_in = _L0_attn_setup()

    def _L0_ffn_setup():
        import jax, jax.numpy as jnp
        import numpy as np
        DIM = 128
        DEPTH = 6
        HEADS = 16
        DIM_HEAD = 64
        WINDOW = 32
        INNER = HEADS * DIM_HEAD
        DIM_INNER = int(DIM * 4 * 2 / 3)
        QK_SCALE = 8.0

        def shift_tokens(t):
            a, s = jnp.split(t, 2, -1)
            s = jnp.pad(s, ((0, 0), (1, 0), (0, 0)))[:, :-1]
            return jnp.concatenate([a, s], -1)

        def l2norm(t):
            return t / jnp.maximum(jnp.linalg.norm(t, axis=-1, keepdims=True), 1e-12)

        def rotate_half(x):
            x1, x2 = jnp.split(x, 2, -1)
            return jnp.concatenate([-x2, x1], -1)

        def rotary_tables(n):
            half = jnp.arange(0, DIM_HEAD, 2, dtype=jnp.float32)
            inv_freq = 1.0 / 10000.0 ** (half / DIM_HEAD)
            t = jnp.arange(n, dtype=jnp.float32)
            freqs = t[:, None] * inv_freq[None, :]
            freqs = jnp.concatenate([freqs, freqs], -1)
            base_scale = (half + 0.4 * DIM_HEAD) / (1.4 * DIM_HEAD)
            power = (t - n // 2) / (WINDOW // 2)
            scale = base_scale[None, :] ** power[:, None]
            scale = jnp.concatenate([scale, scale], -1)
            return (freqs, scale)

        def local_attention(q, k, v):
            b, h, n, d = q.shape
            w = WINDOW
            nw = n // w
            bq = q.reshape(b, h, nw, w, d)
            bk = k.reshape(b, h, nw, w, d)
            bv = v.reshape(b, h, nw, w, d)

            def look(t):
                p = jnp.pad(t, ((0, 0), (0, 0), (1, 0), (0, 0), (0, 0)))
                return jnp.concatenate([p[:, :, :nw], p[:, :, 1:]], axis=3)
            bk2, bv2 = (look(bk), look(bv))
            seq = jnp.arange(n).reshape(nw, w)
            seq_p = jnp.pad(seq, ((1, 0), (0, 0)), constant_values=-1)
            jt = jnp.concatenate([seq_p[:nw], seq_p[1:]], axis=1)
            it = seq[:, :, None]
            jb = jt[:, None, :]
            mask = (it < jb) | (it > jb + w) | (jb == -1)
            sim = jnp.einsum('bhwie,bhwje->bhwij', bq, bk2) * QK_SCALE
            sim = jnp.where(mask, -jnp.finfo(sim.dtype).max, sim)
            attn = jax.nn.softmax(sim, -1)
            out = jnp.einsum('bhwij,bhwje->bhwie', attn, bv2)
            return out.reshape(b, h, n, d)

        def attn_layer(x, Wqkv, qs, ksc, Wo):
            b, n, _ = x.shape
            qkv = x @ Wqkv
            q, k, v = jnp.split(qkv, 3, -1)
            sh = lambda t: t.reshape(b, n, HEADS, DIM_HEAD).transpose(0, 2, 1, 3)
            q, k, v = (sh(q), sh(k), sh(v))
            q = l2norm(q) * qs
            k = l2norm(k) * ksc
            freqs, scale = rotary_tables(n)
            cos, sin = (jnp.cos(freqs), jnp.sin(freqs))
            q = q * cos * scale + rotate_half(q) * sin * scale
            inv = 1.0 / scale
            k = k * cos * inv + rotate_half(k) * sin * inv
            out = local_attention(q, k, v)
            out = out.transpose(0, 2, 1, 3).reshape(b, n, INNER)
            return out @ Wo

        def ffn_layer(x, g, bln, W1, b1, W2, b2):
            mu = x.mean(-1, keepdims=True)
            var = ((x - mu) ** 2).mean(-1, keepdims=True)
            xn = (x - mu) / jnp.sqrt(var + 1e-05) * g + bln
            hg = xn @ W1 + b1
            a, gate = jnp.split(hg, 2, -1)
            return a * jax.nn.gelu(gate, approximate=False) @ W2 + b2
        key = jax.random.key(seed)
        ks = jax.random.split(key, 8)
        B, N = (2, 256)
        init = lambda k, shape: jax.random.normal(k, shape, jnp.float32) * 0.02
        return {'x': jax.random.normal(ks[0], (B, N, DIM), jnp.float32), 'Wqkv': init(ks[1], (DEPTH, DIM, 3 * INNER)), 'q_scale': jnp.ones((DEPTH, DIM_HEAD), jnp.float32), 'k_scale': jnp.ones((DEPTH, DIM_HEAD), jnp.float32), 'Wo': init(ks[2], (DEPTH, INNER, DIM)), 'ln_g': jnp.ones((DEPTH, DIM), jnp.float32), 'ln_b': jnp.zeros((DEPTH, DIM), jnp.float32), 'W1': init(ks[3], (DEPTH, DIM, 2 * DIM_INNER)), 'b1': jnp.zeros((DEPTH, 2 * DIM_INNER), jnp.float32), 'W2': init(ks[4], (DEPTH, DIM_INNER, DIM)), 'b2': jnp.zeros((DEPTH, DIM), jnp.float32)}
    _L0_ffn_in = _L0_ffn_setup()
    _d = {'L0_attn_x': _L0_attn_in['x'], 'L0_attn_A': _L0_attn_in['A'], 'L0_attn_B': _L0_attn_in['B'], 'L0_attn_C': _L0_attn_in['C'], 'L0_attn_gamma': _L0_attn_in['gamma'], 'L0_attn_beta': _L0_attn_in['beta'], 'L0_ffn_Wqkv': _L0_ffn_in['Wqkv'], 'L0_ffn_q_scale': _L0_ffn_in['q_scale'], 'L0_ffn_k_scale': _L0_ffn_in['k_scale'], 'L0_ffn_Wo': _L0_ffn_in['Wo'], 'L0_ffn_ln_g': _L0_ffn_in['ln_g'], 'L0_ffn_ln_b': _L0_ffn_in['ln_b'], 'L0_ffn_W1': _L0_ffn_in['W1'], 'L0_ffn_b1': _L0_ffn_in['b1'], 'L0_ffn_W2': _L0_ffn_in['W2'], 'L0_ffn_b2': _L0_ffn_in['b2']}
    _x0 = _d['L0_attn_x']
    _d['L0_attn_x'] = jax.random.normal(jax.random.fold_in(jax.random.key(seed), 1), (8, 512, 128), dtype=_x0.dtype)
    del _x0
    return _d

def reference(L0_attn_x, L0_attn_A, L0_attn_B, L0_attn_C, L0_attn_gamma, L0_attn_beta, L0_ffn_Wqkv, L0_ffn_q_scale, L0_ffn_k_scale, L0_ffn_Wo, L0_ffn_ln_g, L0_ffn_ln_b, L0_ffn_W1, L0_ffn_b1, L0_ffn_W2, L0_ffn_b2):

    def _L0_attn_ref(x, A, B, C, gamma, beta):
        import jax, jax.numpy as jnp
        import numpy as np
        LN_EPS = 1e-05
        batch, seq_len, d = x.shape
        xb = jnp.einsum('bsd,ed->sbe', x, B)

        def step(h, xb_t):
            h = jnp.tanh(h @ A.T + xb_t)
            y = h @ C.T
            return (h, y)
        h0 = jnp.zeros((batch, d), dtype=x.dtype)
        _, ys = jax.lax.scan(step, h0, xb)
        out = jnp.transpose(ys, (1, 0, 2)) + x
        mu = jnp.mean(out, axis=-1, keepdims=True)
        var = jnp.mean(jnp.square(out - mu), axis=-1, keepdims=True)
        return (out - mu) * jax.lax.rsqrt(var + LN_EPS) * gamma + beta

    def _L0_ffn_ref(x, Wqkv, q_scale, k_scale, Wo, ln_g, ln_b, W1, b1, W2, b2):
        import jax, jax.numpy as jnp
        import numpy as np
        DIM = 128
        DEPTH = 6
        HEADS = 16
        DIM_HEAD = 64
        WINDOW = 32
        INNER = HEADS * DIM_HEAD
        DIM_INNER = int(DIM * 4 * 2 / 3)
        QK_SCALE = 8.0

        def shift_tokens(t):
            a, s = jnp.split(t, 2, -1)
            s = jnp.pad(s, ((0, 0), (1, 0), (0, 0)))[:, :-1]
            return jnp.concatenate([a, s], -1)

        def l2norm(t):
            return t / jnp.maximum(jnp.linalg.norm(t, axis=-1, keepdims=True), 1e-12)

        def rotate_half(x):
            x1, x2 = jnp.split(x, 2, -1)
            return jnp.concatenate([-x2, x1], -1)

        def rotary_tables(n):
            half = jnp.arange(0, DIM_HEAD, 2, dtype=jnp.float32)
            inv_freq = 1.0 / 10000.0 ** (half / DIM_HEAD)
            t = jnp.arange(n, dtype=jnp.float32)
            freqs = t[:, None] * inv_freq[None, :]
            freqs = jnp.concatenate([freqs, freqs], -1)
            base_scale = (half + 0.4 * DIM_HEAD) / (1.4 * DIM_HEAD)
            power = (t - n // 2) / (WINDOW // 2)
            scale = base_scale[None, :] ** power[:, None]
            scale = jnp.concatenate([scale, scale], -1)
            return (freqs, scale)

        def local_attention(q, k, v):
            b, h, n, d = q.shape
            w = WINDOW
            nw = n // w
            bq = q.reshape(b, h, nw, w, d)
            bk = k.reshape(b, h, nw, w, d)
            bv = v.reshape(b, h, nw, w, d)

            def look(t):
                p = jnp.pad(t, ((0, 0), (0, 0), (1, 0), (0, 0), (0, 0)))
                return jnp.concatenate([p[:, :, :nw], p[:, :, 1:]], axis=3)
            bk2, bv2 = (look(bk), look(bv))
            seq = jnp.arange(n).reshape(nw, w)
            seq_p = jnp.pad(seq, ((1, 0), (0, 0)), constant_values=-1)
            jt = jnp.concatenate([seq_p[:nw], seq_p[1:]], axis=1)
            it = seq[:, :, None]
            jb = jt[:, None, :]
            mask = (it < jb) | (it > jb + w) | (jb == -1)
            sim = jnp.einsum('bhwie,bhwje->bhwij', bq, bk2) * QK_SCALE
            sim = jnp.where(mask, -jnp.finfo(sim.dtype).max, sim)
            attn = jax.nn.softmax(sim, -1)
            out = jnp.einsum('bhwij,bhwje->bhwie', attn, bv2)
            return out.reshape(b, h, n, d)

        def attn_layer(x, Wqkv, qs, ksc, Wo):
            b, n, _ = x.shape
            qkv = x @ Wqkv
            q, k, v = jnp.split(qkv, 3, -1)
            sh = lambda t: t.reshape(b, n, HEADS, DIM_HEAD).transpose(0, 2, 1, 3)
            q, k, v = (sh(q), sh(k), sh(v))
            q = l2norm(q) * qs
            k = l2norm(k) * ksc
            freqs, scale = rotary_tables(n)
            cos, sin = (jnp.cos(freqs), jnp.sin(freqs))
            q = q * cos * scale + rotate_half(q) * sin * scale
            inv = 1.0 / scale
            k = k * cos * inv + rotate_half(k) * sin * inv
            out = local_attention(q, k, v)
            out = out.transpose(0, 2, 1, 3).reshape(b, n, INNER)
            return out @ Wo

        def ffn_layer(x, g, bln, W1, b1, W2, b2):
            mu = x.mean(-1, keepdims=True)
            var = ((x - mu) ** 2).mean(-1, keepdims=True)
            xn = (x - mu) / jnp.sqrt(var + 1e-05) * g + bln
            hg = xn @ W1 + b1
            a, gate = jnp.split(hg, 2, -1)
            return a * jax.nn.gelu(gate, approximate=False) @ W2 + b2
        for i in range(DEPTH):
            x = attn_layer(shift_tokens(x), Wqkv[i], q_scale[i], k_scale[i], Wo[i]) + x
            x = ffn_layer(shift_tokens(x), ln_g[i], ln_b[i], W1[i], b1[i], W2[i], b2[i]) + x
        return x
    x = L0_attn_x
    x = x + _L0_attn_ref(_layernorm(x, axis=-1), L0_attn_A, L0_attn_B, L0_attn_C, L0_attn_gamma, L0_attn_beta)
    x = x + _L0_ffn_ref(_layernorm(x, axis=-1), L0_ffn_Wqkv, L0_ffn_q_scale, L0_ffn_k_scale, L0_ffn_Wo, L0_ffn_ln_g, L0_ffn_ln_b, L0_ffn_W1, L0_ffn_b1, L0_ffn_W2, L0_ffn_b2)
    return x

_drawn_inputs = setup_inputs


def setup_inputs(seed=0):
    import zlib

    import numpy as np

    out = dict(_drawn_inputs(seed))
    spreads = {'L0_attn_gamma': (1.0, 0.2),
     'L0_attn_beta': (0.0, 0.1),
     'L0_ffn_q_scale': (1.0, 0.6),
     'L0_ffn_k_scale': (1.0, 0.6),
     'L0_ffn_ln_g': (1.0, 0.6),
     'L0_ffn_ln_b': (0.0, 0.8),
     'L0_ffn_b1': (0.0, 0.8),
     'L0_ffn_b2': (0.0, 0.304)}
    factors = {'L0_attn_A': 8.0,
     'L0_attn_B': 8.0,
     'L0_attn_C': 8.0,
     'L0_ffn_W1': 5.542,
     'L0_ffn_W2': 5.449}
    for name, (base, spread) in spreads.items():
        noise = np.random.default_rng([zlib.crc32(name.encode()), seed]).standard_normal(out[name].shape)
        drawn = base * np.exp(spread * noise) if base else spread * noise
        out[name] = jnp.asarray(drawn.astype(out[name].dtype))
    for name, factor in factors.items():
        out[name] = (out[name] * factor).astype(out[name].dtype)
    return out
```

```python
from contextlib import ExitStack

import numpy as np

import concourse.bass as bass
from concourse import mybir

ALU = mybir.AluOpType
ACT = mybir.ActivationFunctionType
AX_X = mybir.AxisListType.X
F32 = mybir.dt.float32
BF16 = mybir.dt.bfloat16
I32 = mybir.dt.int32

P = 128
BATCH, SEQ, D = 8, 512, 128
DEPTH, HEADS, DH, WIN = 6, 16, 64, 32
INNER = HEADS * DH
FF = int(D * 4 * 2 / 3)
FT = [(0, 128), (128, 128), (256, FF - 256)]
NW = SEQ // WIN
GB = P // WIN
NG = BATCH // GB
TILES = NW * NG
HP = HEADS // 2
ROUND = 4
TURNS = TILES // ROUND
BLK = 64
NBLK = SEQ // BLK
TB = SEQ // P
EPS = 1e-5
MASKED = -1e30
MAGIC = 0x5F3759DF
NEWTON = 3
NSTEPS = 2 + 3 * NEWTON
SCALE = 8.0
SEED_OPS = 2


def rsqrt(eng, x, bits, half, y, sem, base):
    eng.tensor_scalar(bits, x.bitcast(I32), 1, None, ALU.logical_shift_right).then_inc(sem, 1)
    eng.wait_ge(sem, base + 1)
    eng.tensor_scalar(y.bitcast(I32), bits, -1, MAGIC, ALU.mult, ALU.add).then_inc(sem, 1)
    n = 2
    for _ in range(NEWTON):
        eng.wait_ge(sem, base + n)
        eng.tensor_tensor(half, y, y, ALU.mult).then_inc(sem, 1)
        eng.wait_ge(sem, base + n + 1)
        eng.scalar_tensor_tensor(out=half, in0=half, scalar=-0.5, in1=x, op0=ALU.mult, op1=ALU.mult).then_inc(sem, 1)
        eng.wait_ge(sem, base + n + 2)
        eng.scalar_tensor_tensor(out=y, in0=half, scalar=1.5, in1=y, op0=ALU.add, op1=ALU.mult).then_inc(sem, 1)
        n += 3



class Steps:

    def __init__(self, eng, sem, base):
        self.eng, self.sem, self.base, self.n = eng, sem, base, 0

    def __call__(self, ins):
        ins.then_inc(self.sem, 1)
        self.n += 1
        self.eng.wait_ge(self.sem, self.base + self.n)


def layernorm(eng, step, src, dst, c, t4, bits):
    shape = [P, TB, D]
    mean, var, half, r = (t4[:, i, :] for i in range(4))
    step(eng.tensor_reduce(mean, src, AX_X, ALU.add))
    step(eng.tensor_scalar(mean, mean, 1.0 / D, None, ALU.mult))
    step(eng.tensor_tensor(dst, src, mean.unsqueeze(2).to_broadcast(shape), ALU.subtract))
    step(eng.tensor_tensor(c, dst, dst, ALU.mult))
    step(eng.tensor_reduce(var, c, AX_X, ALU.add))
    step(eng.tensor_scalar(var, var, 1.0 / D, EPS, ALU.mult, ALU.add))
    rsqrt(eng, var, bits, half, r, step.sem, step.base + step.n)
    step.n += NSTEPS
    eng.wait_ge(step.sem, step.base + step.n)
    step(eng.tensor_tensor(dst, dst, r.unsqueeze(2).to_broadcast(shape), ALU.mult))


LN_STEPS = 7 + NSTEPS
POST_STEPS = 2 + LN_STEPS + 3 + LN_STEPS
DMA_V = 2 * GB


def build(nc, a):
    with ExitStack() as ctx:
        def sb(name, shape, dt=F32):
            return ctx.enter_context(nc.sbuf_tensor(name, shape, dt))

        def sem(name):
            return ctx.enter_context(nc.semaphore(name))

        ident = sb("ident", [P, P])
        ident_bf = sb("ident_bf", [P, P], BF16)
        ones = sb("ones", [P, P])
        mean_w = sb("mean_w", [P, P])
        mask_f = sb("mask_f", [P, 3, DH])
        mask = sb("mask", [P, 3, DH], BF16)
        x1 = sb("x1", [P, BATCH, TB, D])
        xa = sb("xa", [P, BATCH, 1 + SEQ])
        xb = sb("xb", [P, BATCH, 1 + SEQ])
        w_qkv = sb("w_qkv", [P, 3, INNER])
        w_o = sb("w_o", [P, HP, D])
        w_1 = sb("w_1", [P, 2 * FF])
        w_2 = sb("w_2", [P, 3, D])
        tab = sb("tab", [P, 4, NW * DH])
        qks = sb("qks", [P, 4, DH])
        vec = sb("vec", [P, 9])
        xs = sb("xs", [P, 2, P])
        qk = sb("qk", [P, 2, INNER])
        cosp = sb("cosp", [P, 2, 2, INNER])
        sinp = sb("sinp", [P, 2, INNER])
        sq = sb("sq", [P, 2, INNER])
        ssq = sb("ssq", [P, 2 * HEADS])
        rbits = sb("rbits", [P, 2 * HEADS], I32)
        rhalf = sb("rhalf", [P, 2 * HEADS])
        rtmp = sb("rtmp", [P, 2 * HEADS])
        rnorm = sb("rnorm", [P, 2 * HEADS])
        qT = sb("qT", [P, HP, P])
        kT = sb("kT", [P, NG, HP, GB, 2 * WIN])
        sh = sb("sh", [P, INNER])
        ex = sb("ex", [P, INNER])
        mx = sb("mx", [P, HEADS])
        esum = sb("esum", [P, HEADS])
        rsum = sb("rsum", [P, HEADS])
        aT = sb("aT", [P, 8, P])
        vt = sb("vt", [P, 2, 2, 512])
        vk = sb("vk", [P, NG, GB, 512])
        on = sb("on", [P, INNER])
        oT = sb("oT", [P, HP, P])
        CH = BATCH * WIN
        room = cosp.rearrange("p a b n -> p (a b n)")
        xc, cc, cq, xn, xf = (room[:, i * CH:(i + 1) * CH] for i in range(5))
        ge = room[:, 5 * CH:8 * CH].rearrange("p (m n) -> p m n", m=3)
        hh = room[:, 8 * CH:11 * CH].rearrange("p (m n) -> p m n", m=3)
        dg = room[:, 11 * CH:12 * CH]
        xf2 = (xf, room[:, 12 * CH:13 * CH])
        fx = sb("fx", [P, 2])
        fbits = sb("fbits", [P, 2], I32)
        fhalf = sb("fhalf", [P, 2])
        fr = sb("fr", [P, 2])
        xnt = tab.rearrange("p a (b n) -> p (a b) n", b=2).rearrange("p b (j d) -> p b j d", j=TB)
        xnf = kT.rearrange("p g h b k -> p (g h b k)").rearrange("p (b t) -> p b t", b=BATCH)
        hall = vk.rearrange("p g b n -> p (g b) n")
        hb = cosp.rearrange("p a b n -> p (a b n)")[:, 0:2 * BLK * BATCH].rearrange("p (r t b) -> p r t b", r=2, b=BATCH)
        lnc = sq.rearrange("p a n -> p (a n)")[:, 0:512].rearrange("p (j d) -> p j d", j=TB)
        lnd = sinp.rearrange("p a n -> p (a n)")[:, 0:512].rearrange("p (j d) -> p j d", j=TB)
        lno = on[:, 0:512].rearrange("p (j d) -> p j d", j=TB)
        hs = oT[:, 0:TB, :]
        abc = qT[:, 0:3, :]
        abcT = qT[:, 3:6, :]
        gam = aT[:, 0, :]
        bet = aT[:, 1, :]
        t4 = sb("t4", [P, 4, TB])
        b4 = sb("b4", [P, TB], I32)
        fin = sb("fin", [P, 2, TB, D])
        ps = ctx.enter_context(nc.psum_tensor("ps", [P, 8, 512], F32))

        consts_in = sem("consts_in")
        x_in = sem("x_in")
        zeroed = sem("zeroed")
        abc_in = sem("abc_in")
        abc_turned = sem("abc_turned")
        abc_out = sem("abc_out")
        ln1_step = sem("ln1_step")
        ln1_turned = sem("ln1_turned")
        ln1_out = sem("ln1_out")
        pre_done = sem("pre_done")
        h_done = sem("h_done")
        hall_done = sem("hall_done")
        post_step = sem("post_step")
        hs_turned = sem("hs_turned")
        post_turned = sem("post_turned")
        xa_out = sem("xa_out")
        qkv_in = sem("qkv_in")
        tables_in = sem("tables_in")
        tables_ready = sem("tables_ready")
        wo_in = sem("wo_in")
        ffn_in = sem("ffn_in")
        xs_ready = sem("xs_ready")
        proj_done = sem("proj_done")
        r_evac = sem("r_evac")
        rot_done = sem("rot_done")
        sq_done = sem("sq_done")
        ssq_done = sem("ssq_done")
        norm_step = sem("norm_step")
        rot_added = sem("rot_added")
        rot_ready = sem("rot_ready")
        qkT_done = sem("qkT_done")
        qk_evac = sem("qk_evac")
        sims_done = sem("sims_done")
        max_done = sem("max_done")
        centered = sem("centered")
        exp_done = sem("exp_done")
        rsum_done = sem("rsum_done")
        recip_done = sem("recip_done")
        aT_done = sem("aT_done")
        at_evac = sem("at_evac")
        pv_done = sem("pv_done")
        o_read = sem("o_read")
        oT_done = sem("oT_done")
        ot_evac = sem("ot_evac")
        y_done = sem("y_done")
        y_added = sem("y_added")
        xc_ready = sem("xc_ready")
        mean_done = sem("mean_done")
        ctr_done = sem("ctr_done")
        csq_done = sem("csq_done")
        var_done = sem("var_done")
        fnorm_step = sem("fnorm_step")
        bc_done = sem("bc_done")
        xn_done = sem("xn_done")
        affine_done = sem("affine_done")
        hg_done = sem("hg_done")
        gelu_done = sem("gelu_done")
        glu_done = sem("glu_done")
        fy_done = sem("fy_done")
        x_updated = sem("x_updated")
        end_read = sem("end_read")
        end_turned = sem("end_turned")
        end_added = sem("end_added")
        out_done = sem("out_done")
        out_done2 = sem("out_done2")
        mask_in = sem("mask_in")

        from_one = (
            r_evac, proj_done, rot_done, y_done, y_added, x_updated, ssq_done, sq_done, norm_step, sims_done,
            centered, exp_done, rsum_done, recip_done, aT_done, pv_done, o_read, oT_done, glu_done, xn_done,
            ctr_done, fy_done, fnorm_step, bc_done, affine_done, h_done, hall_done, ln1_step, post_step,
            ln1_out, post_turned, xa_out, end_added, end_turned, at_evac, rot_added, rot_ready, qk_evac,
            ot_evac,
        )

        def settled(eng):
            eng.sem_inc(carried[eng.engine.name], 1)

        carried = {n: sem("carried_" + n) for n in ("PE", "DVE", "Activation", "Pool")}
        v_landed = [sem(f"v_landed{i}") for i in range(ROUND)]
        block = ctx.enter_context(nc.Block())

        R = lambda n: ps[:, n % 2, :]
        T = lambda n: ps[:, 2 + n % 2, :]
        scores = ps[:, 4:6, :].rearrange("p a (h k) -> p (a h) k", k=DH)
        O = lambda x: ps[:, 6 + x, :]

        def attention_steps(eng, L, step, head=0):
            steps = TILES + 3
            for s in range(ROUND):
                step(s, L * TILES + s, L * TURNS, s)
            with eng.Fori(1, TURNS) as it:
                g0 = eng.snap(L * TILES + it * ROUND)
                q0 = eng.snap(L * TURNS + it)
                for j in range(ROUND):
                    step(j, g0 + j, q0, None, it)
            for s in range(TILES, steps):
                step(s % ROUND, L * TILES + s, L * TURNS + TURNS, s)

        def active(s, back):
            return s is None or 0 <= s - back < TILES

        @block.sync
        def _(eng):
            for name, dst in (("ident", ident[:, :]), ("mask", mask_f[:, :, :])):
                eng.dma_start(dst, a[name]).then_inc(consts_in, 16)
            for i, name in enumerate("ABC"):
                eng.dma_start(abc[:, i, :], a["L0_attn_" + name]).then_inc(abc_in, 16)
            for name, dst in (("L0_attn_gamma", gam), ("L0_attn_beta", bet)):
                eng.dma_start(dst, a[name].rearrange("(o d) -> o d", o=1).to_broadcast([P, D])).then_inc(abc_in, 16)
            for b in range(BATCH):
                eng.dma_start(x1[:, b, :, :], a["L0_attn_x"][b].rearrange("(j p) d -> p j d", p=P)).then_inc(x_in, 16)
            for signal in from_one:
                eng.sem_inc(signal, 1)
            with eng.Fori(0, DEPTH) as L:
                eng.wait_ge(proj_done, L * (6 * TILES) + 1)
                eng.dma_start(w_qkv[:, :, :].rearrange("p a n -> p (a n)"),
                              a["L0_ffn_Wqkv"][bass.ds(L, 1), :, :].rearrange("o p n -> (o p) n")).then_inc(qkv_in, 16)
                eng.wait_ge(rot_done, L * (4 * TILES) + 1)
                eng.wait_ge(post_step, POST_STEPS * BATCH + 1)
                eng.dma_start(tab[:, :, :], a["tab"]).then_inc(tables_in, 16)
                for i, name in ((0, "q"), (2, "k")):
                    src = a[f"L0_ffn_{name}_scale"][bass.ds(L, 1), :]
                    eng.dma_start(qks[:, i, :], src.to_broadcast([P, DH])).then_inc(tables_in, 16)
                    for u in range(2):
                        half = a[f"L0_ffn_{name}_scale"][bass.ds(L, 1), 32 * (1 - u):32 * (1 - u) + 32]
                        eng.dma_start(qks[:, i + 1, 32 * u:32 * u + 32], half.to_broadcast([P, 32])).then_inc(tables_in, 16)
                eng.wait_ge(y_done, L * TILES + 1)
                eng.dma_start(w_o[:, :, :], a["L0_ffn_Wo"][bass.ds(L, 1), :, :].rearrange("o (k p) n -> p (o k) n", p=P)).then_inc(wo_in, 16)
                eng.wait_ge(x_updated, L * NW + 1)
                eng.dma_start(w_1[:, :], a["L0_ffn_W1"][bass.ds(L, 1), :, :].rearrange("o p n -> (o p) n")).then_inc(ffn_in, 16)
                for m, (f0, fn) in enumerate(FT):
                    eng.dma_start(w_2[0:fn, m, :], a["L0_ffn_W2"][bass.ds(L, 1), f0:f0 + fn, :].rearrange("o p n -> (o p) n")).then_inc(ffn_in, 16)
                for i, name in enumerate(("ln_g", "ln_b", "b2")):
                    eng.dma_start(vec[:, i:i + 1], a["L0_ffn_" + name][bass.ds(L, 1), :].rearrange("o p -> p o")).then_inc(ffn_in, 16)
                for u in range(2):
                    for m, (f0, fn) in enumerate(FT):
                        eng.dma_start(vec[0:fn, 3 + 3 * u + m:4 + 3 * u + m],
                                      a["L0_ffn_b1"][bass.ds(L, 1), u * FF + f0:u * FF + f0 + fn].rearrange("o p -> p o")).then_inc(ffn_in, 16)

                def step(j, G, Q, s, it=None):
                    if not active(s, 0):
                        return
                    g, slot = j % 2, j // 2
                    eng.wait_ge(r_evac, G * 6 + 7)
                    if s is None or s >= 2:
                        eng.wait_ge(pv_done, G)
                    for x in range(2):
                        for b in range(GB):
                            eng.dma_start(vk[64 * x + 32 * slot:64 * x + 32 * slot + 32, g, b, :],
                                          vt[32 * b:32 * b + 32, j % 2, x, :]).then_inc(v_landed[j], 16)

                attention_steps(eng, L, step)
            for b in range(BATCH):
                eng.wait_ge(end_added, b + 2)
                eng.dma_start(a["out"][b].rearrange("(j p) d -> p j d", p=P), fin[:, b % 2, :, :]).then_inc((out_done2 if b % 2 else out_done), 16)
            eng.wait_ge(out_done, 16 * BATCH // 2)
            eng.wait_ge(out_done2, 16 * BATCH // 2)

        @block.gpsimd
        def _(eng):
            eng.memset(ones[:, :], 1.0).then_inc(zeroed, 1)
            eng.memset(mean_w[:, :], 1.0 / D).then_inc(zeroed, 1)
            eng.memset(xa[:, :, 0:1], 0.0).then_inc(zeroed, 1)
            eng.memset(xb[:, :, 0:1], 0.0).then_inc(zeroed, 1)
            eng.memset(hb[:, 1, BLK - 1, :], 0.0).then_inc(zeroed, 1)
            with eng.Fori(0, NBLK // 2) as it:
                for r in range(2):
                    eng.wait_ge(h_done, it * (2 * BLK) + (r + 1) * BLK + 1)
                    eng.tensor_copy(hall[:, :, bass.ds(it * (2 * BLK) + r * BLK, BLK)],
                                    hb[:, r, :, :].rearrange("p t b -> p b t")).then_inc(hall_done, 1)
            with eng.Fori(0, DEPTH) as L:
                eng.wait_ge(tables_in, L * (16 * 7) + 16 * 7)
                for i in range(4):
                    t = tab[:, i, :].rearrange("p (w d) -> p w d", d=DH)
                    eng.tensor_tensor(t, t, qks[:, i, :].unsqueeze(1).to_broadcast([P, NW, DH]), ALU.mult).then_inc(tables_ready, 1)
                def step(j, G, Q, s, it=None):
                    if active(s, 1):
                        r, g1 = (j - 1) % 2, G - 1
                        for i in range(2):
                            eng.wait_ge(rot_done, g1 * 4 + 2 * i + 3)
                            eng.tensor_tensor(cosp[:, r, i, :], cosp[:, r, i, :], sinp[:, i, :], ALU.add).then_inc(rot_added, 1)
                        eng.wait_ge(norm_step, g1 * (NSTEPS + 2) + NSTEPS + 3)
                        for i in range(2):
                            eng.wait_ge(rot_added, g1 * 2 + i + 2)
                            v = cosp[:, r, i, :].rearrange("p (h d) -> p h d", d=DH)
                            eng.tensor_tensor(v, v, rnorm[:, HEADS * i:HEADS * i + HEADS].unsqueeze(2).to_broadcast([P, HEADS, DH]),
                                              ALU.mult).then_inc(rot_ready, 1)

                attention_steps(eng, L, step)


        @block.tensor
        def _(eng):
            eng.wait_ge(abc_in, 16 * 5)
            eng.wait_ge(consts_in, 32)
            for i in range(3):
                eng.transpose(ps[:, 0, 128 * i:128 * i + 128], abc[:, i, :], ident[:, :]).then_inc(abc_turned, 1)
            with eng.Fori(0, BATCH) as b:
                eng.wait_ge(ln1_step, b * LN_STEPS + LN_STEPS + 1)
                eng.wait_ge(ln1_out, b * 2 + 1)
                for j in range(TB):
                    t = eng.transpose(ps[:, 1, 128 * j:128 * j + 128], lnd[:, j, :], ident[:, :])
                t.then_inc(ln1_turned, 1)
            eng.wait_ge(ln1_out, 2 * BATCH + 1)
            eng.wait_ge(abc_out, 1)
            eng.wait_ge(zeroed, 5)
            with eng.Fori(0, NBLK // 2) as it:
                for r in range(2):
                    h0 = it * (2 * BLK) + r * BLK
                    eng.wait_ge(h_done, h0 + 1)
                    settled(eng)
                    eng.matmul(ps[:, r, :], abcT[:, 1, :], xnf[:, :, bass.ds(h0, BLK)].rearrange("p b t -> p t b"),
                               start=True, stop=False, skip_group_check=True)
                    for t in range(BLK):
                        if t:
                            eng.wait_ge(h_done, h0 + t + 1)
                        prev = hb[:, r, t - 1, :] if t else hb[:, 1 - r, BLK - 1, :]
                        eng.matmul(ps[:, r, BATCH * t:BATCH * t + BATCH], abcT[:, 0, :], prev, start=False, stop=t == BLK - 1,
                                   skip_group_check=True).then_inc(pre_done, 1)
            with eng.Fori(0, BATCH) as b:
                eng.wait_ge(post_step, b * POST_STEPS + 2)
                for j in range(TB):
                    t = eng.matmul(ps[:, 2, 128 * j:128 * j + 128], hs[:, j, :], abcT[:, 2, :], start=True, stop=True)
                t.then_inc(hs_turned, 1)
                eng.wait_ge(post_step, b * POST_STEPS + POST_STEPS + 1)
                eng.wait_ge(xa_out, b + 1)
                for j in range(TB):
                    t = eng.transpose(ps[:, 3, 128 * j:128 * j + 128], lnd[:, j, :], ident[:, :])
                t.then_inc(post_turned, 1)
            with eng.Fori(0, DEPTH) as L:
                eng.wait_ge(qkv_in, L * 16 + 16)
                eng.wait_ge(x_updated, L * NW + 1)
                eng.wait_ge(xa_out, BATCH + 1)

                def t_slot(n):
                    return ps[:, 2 + n % 2, :]

                def step(j, G, Q, s, it=None):
                    g1, g2, g3 = (G - 1), (G - 2), (G - 3)
                    if active(s, 0):
                        eng.wait_ge(xs_ready, G * 2 + 2)
                        for c in range(6):
                            if c == 1 and (s is None or s >= 4):
                                eng.wait_ge(y_added, G - 2)
                            if c >= 2:
                                eng.wait_ge(r_evac, G * 6 + c)
                            elif c == 0:
                                eng.wait_ge(r_evac, G * 6 + 1)
                            n, i = 7 * j + c, c // 2
                            if i < 2:
                                w = w_qkv[:, i, 512 * (c % 2):512 * (c % 2) + 512]
                            else:
                                w = w_qkv[:, 2, :].rearrange("p (m x h d) -> p x h m d", m=4, x=2, h=2)[:, c % 2]
                            eng.matmul(R(n), xs[:, j % 2, :], w, start=True, stop=True).then_inc(proj_done, 1)
                    if active(s, 3):
                        for u in range(2):
                            eng.wait_ge(o_read, g3 * 2 + 3)
                            eng.wait_ge(at_evac, g3 * 2 + 1 + u + 1)
                            for k in range(4):
                                t = eng.transpose(t_slot(u)[:, 128 * k:128 * k + 128], on[:, 512 * u + 128 * k:512 * u + 128 * k + 128], ident[:, :])
                            t.then_inc(oT_done, 1)
                        if not active(s, 0):
                            eng.wait_ge(r_evac, L * (6 * TILES) + 6 * TILES + 1)
                            if s > TILES:
                                eng.wait_ge(y_added, g3 + 1)
                        else:
                            eng.wait_ge(r_evac, G * 6 + 6)
                        if s is not None and s == 3:
                            eng.wait_ge(wo_in, L * 16 + 16)
                        eng.wait_ge(ot_evac, g3 * 2 + 3)
                        for k in range(HP):
                            t = eng.matmul(R(7 * j + 6)[:, 0:P], w_o[:, k, :], oT[:, k, :], start=k == 0, stop=k == HP - 1)
                        t.then_inc(y_done, 1)
                    if active(s, 1):
                        gg, slot = (j - 1) % 2, ((j - 1) % ROUND) // 2
                        for i in range(2):
                            eng.wait_ge(rot_ready, g1 * 2 + 1 + i + 1)
                            for u in range(2):
                                if i == 0:
                                    if active(s, 3):
                                        eng.wait_ge(ot_evac, g3 * 2 + 1 + u + 1)
                                    elif s == 2:
                                        eng.wait_ge(qk_evac, g1 * 4 - 1 + u + 1)
                                else:
                                    eng.wait_ge(qk_evac, g1 * 4 + 1 + u + 1)
                                for k in range(4):
                                    hp = 4 * u + k
                                    t = eng.transpose(t_slot(u)[:, 128 * k:128 * k + 128], cosp[:, (j - 1) % 2, i, 128 * hp:128 * hp + 128], ident[:, :])
                                t.then_inc(qkT_done, 1)
                        eng.wait_ge(centered, g1 + 1)
                        eng.wait_ge(mask_in, 2)
                        variant = 2 if s is not None and s - 1 < 2 else slot
                        for h2 in range(2):
                            eng.matmul(ps[:, 4 + h2, :].rearrange("p (h k) -> p h k", k=DH), ident_bf[:, :],
                                       mask[:, variant, :].unsqueeze(1).to_broadcast([P, 8, DH]), start=True, stop=False, skip_group_check=True)
                        eng.wait_ge(qk_evac, g1 * 4 + 5)
                        settled(eng)
                        for h2 in range(2):
                            rows = slice(64 * h2, 64 * h2 + 64)
                            for hp in range(HP):
                                for b in range(GB):
                                    t = eng.matmul(ps[32 * b:32 * b + 32, 4 + h2, DH * hp:DH * hp + DH], qT[rows, hp, 32 * b:32 * b + 32],
                                                   kT[rows, gg, hp, b, :], start=False, stop=hp == HP - 1, skip_group_check=True)
                        t.then_inc(sims_done, 1)
                    if active(s, 2):
                        gg = j % 2
                        eng.wait_ge(exp_done, g2 + 2)
                        for u in range(2):
                            if active(s, 1):
                                eng.wait_ge(qk_evac, g1 * 4 + 3 + u + 1)
                            else:
                                eng.wait_ge(ot_evac, g3 * 2 + 1 + u + 1)
                            for k in range(4):
                                t = eng.transpose(t_slot(u)[:, 128 * k:128 * k + 128], ex[:, 512 * u + 128 * k:512 * u + 128 * k + 128], ident[:, :])
                            t.then_inc(aT_done, 1)
                        eng.wait_ge(at_evac, g2 * 2 + 3)
                        eng.wait_ge(o_read, g2 * 2 + 1)
                        d4 = (j - 2) // ROUND
                        eng.wait_ge(v_landed[(j - 2) % ROUND], (Q + (d4 + 1)) * (16 * DMA_V))
                        settled(eng)
                        for x in range(2):
                            rows = slice(64 * x, 64 * x + 64)
                            for k in range(8):
                                for b in range(GB):
                                    t = eng.matmul(ps[32 * b:32 * b + 32, 6 + x, DH * k:DH * k + DH], aT[rows, k, 32 * b:32 * b + 32],
                                                   vk[rows, gg, b, DH * k:DH * k + DH], start=True, stop=True)
                        t.then_inc(pv_done, 1)

                attention_steps(eng, L, step)

                eng.wait_ge(y_added, L * TILES + TILES + 1)
                eng.wait_ge(ffn_in, L * (16 * 13) + 16 * 13)

                def ffn(C, has_a, has_b, has_c, first_b=False):
                    if has_c:
                        c2 = C - 2
                        eng.wait_ge(glu_done, c2 * 3 + 4)
                        eng.wait_ge(x_updated, c2 + 1)
                        for m, (f0, fn) in enumerate(FT):
                            t = eng.matmul(ps[:, 5, 0:CH], w_2[0:fn, m, :], hh[0:fn, m, :], start=m == 0, stop=m == 2)
                        t.then_inc(fy_done, 1)
                    if has_a:
                        eng.wait_ge(xc_ready, C * 2 + 2)
                        eng.wait_ge(ctr_done, C + 1)
                        eng.matmul(ps[:, 0, 0:CH], mean_w[:, :], xc, start=True, stop=True).then_inc(mean_done, 1)
                    c1 = C - 1
                    if has_b:
                        eng.wait_ge(affine_done, c1 + 2)

                    def w1(m):
                        if has_b:
                            f0, fn = FT[m]
                            if not first_b:
                                eng.wait_ge(glu_done, c1 * 3 - 2 + m + 1)
                            for u in (1, 0):
                                t = eng.matmul(ps[0:fn, 2 + m, 256 * u:256 * u + 256], w_1[:, u * FF + f0:u * FF + f0 + fn], xf,
                                               start=True, stop=True)
                            t.then_inc(hg_done, 1)

                    w1(0)
                    if has_a:
                        eng.wait_ge(csq_done, C + 1)
                        eng.wait_ge(xn_done, C + 1)
                        for g in range(2):
                            t = eng.matmul(ps[:, 1, g:g + 1], cq[:, 128 * g:128 * g + 128], mean_w[:, 0:1], start=True, stop=True)
                        t.then_inc(var_done, 1)
                    w1(1)
                    w1(2)
                    if has_a:
                        eng.wait_ge(fnorm_step, C * (NSTEPS + 3) + NSTEPS + 4)
                        eng.matmul(ps[:, 1, 128:128 + CH], ones[:, :], dg, start=True, stop=True).then_inc(bc_done, 1)

                ffn(L * NW, True, False, False)
                ffn(L * NW + 1, True, True, False, True)
                with eng.Fori(2, NW) as c:
                    ffn(eng.snap(L * NW + c), True, True, True)
                ffn(L * NW + NW, False, True, True)
                ffn(L * NW + NW + 1, False, False, True)
            with eng.Fori(0, BATCH) as b:
                eng.wait_ge(end_read, b + 1)
                eng.wait_ge(end_added, b + 1)
                for j in range(TB):
                    t = eng.transpose(ps[:, 0, 128 * j:128 * j + 128], hs[:, j, :], ident[:, :])
                t.then_inc(end_turned, 1)

        @block.scalar
        def _(eng):
            eng.wait_ge(abc_turned, 3)
            eng.copy(abcT.rearrange("p a n -> p (a n)"), ps[:, 0, 0:384]).then_inc(abc_out, 1)
            with eng.Fori(0, BATCH) as b:
                eng.wait_ge(ln1_step, b * LN_STEPS + LN_STEPS + 1)
                eng.copy(xnt[:, bass.ds(b, 1), :, :].rearrange("p o j d -> p (o j) d"), lnd).then_inc(ln1_out, 1)
                eng.wait_ge(ln1_turned, b + 1)
                eng.copy(xnf[:, bass.ds(b, 1), :].rearrange("p o t -> p (o t)"), ps[:, 1, :]).then_inc(ln1_out, 1)
            with eng.Fori(0, NBLK // 2) as it:
                for r in range(2):
                    h0 = it * (2 * BLK) + r * BLK
                    for t in range(BLK):
                        eng.wait_ge(pre_done, h0 + t + 1)
                        if t == 0:
                            eng.wait_ge(hall_done, (it * 2 + r - 1 if r else it * 2) + 1)
                        eng.activation(hb[:, r, t, :], ps[:, r, BATCH * t:BATCH * t + BATCH], ACT.Tanh).then_inc(h_done, 1)
            with eng.Fori(0, BATCH) as b:
                eng.wait_ge(post_turned, b + 2)
                eng.copy(xa[:, bass.ds(b, 1), 1:1 + SEQ].rearrange("p o t -> p (o t)"), ps[:, 3, :]).then_inc(xa_out, 1)
            with eng.Fori(0, DEPTH) as L:
                eng.wait_ge(x_updated, L * NW + 1)

                def shifted(dst, src, batches, col, signal):
                    for h in range(2):
                        rows = slice(64 * h, 64 * h + 64)
                        cols = slice(col + 1 - h, col + 1 - h + WIN) if isinstance(col, int) else bass.ds(col + (1 - h), WIN)
                        eng.copy(dst[rows], src[rows, batches, cols]).then_inc(signal, 1)

                def step(j, G, Q, s, it=None):
                    g1, g2, g3 = (G - 1), (G - 2), (G - 3)
                    if active(s, 0):
                        if s is None or s >= 2:
                            eng.wait_ge(proj_done, G * 6 - 5)
                        col = 32 * (s // 2) if s is not None else it * (2 * WIN) + 32 * (j // 2)
                        settled(eng)
                        shifted(xs[:, j % 2, :].rearrange("p (b t) -> p b t", b=GB), xa, slice(GB * (j % 2), GB * (j % 2) + GB), col, xs_ready)
                        for c in range(6):
                            eng.wait_ge(proj_done, G * 6 + c + 2)
                            i = c // 2
                            if c in (0, 2):
                                if c == 0:
                                    eng.wait_ge(sq_done, G * 2 + 1)
                                eng.wait_ge(rot_done, (G * 4 - 2 + 2 * i if not (s == 0) else L * (4 * TILES)) + 1)
                            if c == 4 and (s is None or s >= 2):
                                d4 = (j - 2) // ROUND
                                eng.wait_ge(v_landed[(j - 2) % ROUND], (Q + (d4 + 1)) * (16 * DMA_V))
                            dst = qk[:, i, 512 * (c % 2):512 * (c % 2) + 512] if i < 2 else vt[:, j % 2, c % 2, :]
                            eng.copy(dst, R(7 * j + c)).then_inc(r_evac, 1)
                    if active(s, 3):
                        for u in range(2):
                            eng.wait_ge(oT_done, g3 * 2 + 1 + u + 1)
                            if u == 0:
                                eng.wait_ge(y_done, g3 + 1)
                            eng.copy(oT[:, 4 * u:4 * u + 4, :].rearrange("p a n -> p (a n)"), T(u)).then_inc(ot_evac, 1)
                    if active(s, 0):
                        for i in range(2):
                            eng.wait_ge(ssq_done, (G * 2 - 1 + i if not (s == 0 and i == 0) else L * (2 * TILES)) + 1)
                            eng.wait_ge(r_evac, G * 6 + 2 + 2 * i + 1)
                            eng.activation(sq[:, i, :], qk[:, i, :], ACT.Square).then_inc(sq_done, 1)
                    if active(s, 1):
                        gg, slot = (j - 1) % 2, ((j - 1) % ROUND) // 2
                        eng.wait_ge(sims_done, g1 + 1)
                        for u in range(2):
                            eng.wait_ge(qkT_done, g1 * 4 + 1 + u)
                            eng.copy(qT[:, 4 * u:4 * u + 4, :].rearrange("p a n -> p (a n)"), T(u)).then_inc(qk_evac, 1)
                        for u in range(2):
                            eng.wait_ge(qkT_done, g1 * 4 + 3 + u)
                            dst = kT[:, gg, 4 * u:4 * u + 4, :, 32 * slot:32 * slot + 32]
                            eng.copy(dst, T(u).rearrange("p (h b t) -> p h b t", h=4, b=GB)).then_inc(qk_evac, 1)
                    if active(s, 2):
                        eng.wait_ge(pv_done, g2 + 1)
                        for u in range(2):
                            eng.wait_ge(aT_done, g2 * 2 + 1 + u + 1)
                            eng.copy(aT[:, 4 * u:4 * u + 4, :].rearrange("p a n -> p (a n)"), T(u)).then_inc(at_evac, 1)
                    if active(s, 1):
                        eng.wait_ge(centered, g1 + 2)
                        eng.wait_ge(rsum_done, g1 + 1)
                        eng.wait_ge(aT_done, g1 * 2 + 1)
                        eng.activation(ex[:, :], sh[:, :], ACT.Exp, scale=SCALE).then_inc(exp_done, 1)

                attention_steps(eng, L, step)
                eng.wait_ge(ffn_in, L * (16 * 13) + 16 * 13)

                def ffn(C, has_a, has_b, col=None):
                    c1 = C - 1
                    if has_a:
                        eng.wait_ge(y_added, L * TILES + TILES + 1)
                        eng.wait_ge(ctr_done, C + 1)
                        settled(eng)
                        shifted(xc.rearrange("p (b t) -> p b t", b=BATCH), xb, slice(0, BATCH), col, xc_ready)

                    def gelu(m):
                        if has_b:
                            fn = FT[m][1]
                            eng.wait_ge(hg_done, c1 * 3 + m + 1)
                            eng.wait_ge(glu_done, (c1 * 3 - 2 + m if has_b == 2 else L * (3 * NW)) + 1)
                            eng.activation(ge[0:fn, m, :], ps[0:fn, 2 + m, 256:512], ACT.Gelu, bias=vec[0:fn, 6 + m:7 + m]).then_inc(gelu_done, 1)

                    if has_a:
                        eng.wait_ge(ctr_done, C + 2)
                        eng.activation(cq, cc, ACT.Square).then_inc(csq_done, 1)
                    gelu(0)
                    gelu(1)
                    gelu(2)
                    if has_a:
                        eng.wait_ge(xn_done, C + 2)
                        eng.activation(xf, xn, ACT.Identity, bias=vec[:, 1:2], scale=vec[:, 0:1]).then_inc(affine_done, 1)

                ffn(L * NW, True, 0, 0)
                ffn(L * NW + 1, True, 1, WIN)
                with eng.Fori(2, NW) as c:
                    ffn(eng.snap(L * NW + c), True, 2, c * WIN)
                ffn(L * NW + NW, False, 2)

        @block.vector
        def _(eng):
            eng.wait_ge(consts_in, 32)
            eng.tensor_copy(ident_bf[:, :], ident[:, :]).then_inc(mask_in, 1)
            eng.tensor_copy(mask[:, :, :], mask_f[:, :, :]).then_inc(mask_in, 1)
            eng.wait_ge(x_in, 16 * BATCH)
            with eng.Fori(0, BATCH) as b:
                eng.wait_ge(ln1_out, b * 2 + 1)
                settled(eng)
                step = Steps(eng, ln1_step, b * LN_STEPS + 1)
                layernorm(eng, step, x1[:, bass.ds(b, 1), :, :].rearrange("p o j d -> p (o j) d"), lnd, lnc, t4, b4[:, :])
                assert step.n == LN_STEPS
            eng.wait_ge(hall_done, NBLK + 1)
            eng.wait_ge(abc_in, 16 * 5)
            with eng.Fori(0, BATCH) as b:
                row = x1[:, bass.ds(b, 1), :, :].rearrange("p o j d -> p (o j) d")
                step = Steps(eng, post_step, b * POST_STEPS + 1)
                eng.wait_ge(post_turned, b + 1)
                step(eng.tensor_copy(hs.rearrange("p a n -> p (a n)"), hall[:, bass.ds(b, 1), :].rearrange("p o t -> p (o t)")))
                eng.wait_ge(hs_turned, b + 1)
                step(eng.tensor_tensor(lno, ps[:, 2, :].rearrange("p (j d) -> p j d", j=TB),
                                       xnt[:, bass.ds(b, 1), :, :].rearrange("p o j d -> p (o j) d"), ALU.add))
                layernorm(eng, step, lno, lnd, lnc, t4, b4[:, :])
                step(eng.tensor_tensor(lnd, lnd, gam.unsqueeze(1).to_broadcast([P, TB, D]), ALU.mult))
                step(eng.tensor_tensor(lnd, lnd, bet.unsqueeze(1).to_broadcast([P, TB, D]), ALU.add))
                step(eng.tensor_tensor(row, row, lnd, ALU.add))
                settled(eng)
                layernorm(eng, step, row, lnd, lnc, t4, b4[:, :])
                assert step.n == POST_STEPS
            with eng.Fori(0, DEPTH) as L:
                eng.wait_ge(tables_ready, L * 4 + 4)

                def step(j, G, Q, s, it=None):
                    g1, g2, g3 = (G - 1), (G - 2), (G - 3)
                    if active(s, 3):
                        eng.wait_ge(pv_done, g3 + 2)
                        eng.wait_ge(recip_done, g3 + 2)
                        eng.wait_ge(oT_done, g3 * 2 + 1)
                        for x in range(2):
                            dst = on[:, :].rearrange("p (m x h d) -> p x h m d", m=4, x=2, h=2)[:, x]
                            src = O(x).rearrange("p (h m d) -> p h m d", h=2, m=4)
                            r = rsum[:, :].rearrange("p (h m x) -> p x h m", h=2, x=2)[:, x].unsqueeze(3).to_broadcast([P, 2, 4, DH])
                            eng.tensor_tensor(dst, src, r, ALU.mult).then_inc(o_read, 1)
                    if active(s, 2):
                        eng.wait_ge(exp_done, g2 + 2)
                        eng.wait_ge(recip_done, g2 + 1)
                        eng.tensor_reduce(esum[:, :], ex[:, :].rearrange("p (h k) -> p h k", k=DH), AX_X, ALU.add).then_inc(rsum_done, 1)
                        eng.wait_ge(rsum_done, g2 + 2)
                        if active(s, 3):
                            eng.wait_ge(o_read, g3 * 2 + 3)
                        eng.reciprocal(rsum[:, :], esum[:, :]).then_inc(recip_done, 1)
                    if active(s, 3):
                        g = (j - 3) % 2
                        eng.wait_ge(y_done, g3 + 2)
                        if s is not None:
                            col = 1 + 32 * ((s - 3) // 2)
                            cols = slice(col, col + WIN)
                        else:
                            cols = bass.ds(it * (2 * WIN) + (1 + 32 * ((j - 3) // 2)), WIN)
                        eng.tensor_tensor(xb[:, GB * g:GB * g + GB, cols], R(7 * j + 6)[:, 0:P].rearrange("p (b t) -> p b t", b=GB),
                                          xa[:, GB * g:GB * g + GB, cols], ALU.add).then_inc(y_added, 1)
                    if active(s, 0):
                        r = j % 2
                        for i in range(2):
                            src = qk[:, i, :].rearrange("p (h d) -> p h d", d=DH)
                            if s is not None:
                                w = slice(DH * (s // 2), DH * (s // 2) + DH)
                            else:
                                w = bass.ds(it * (2 * DH) + DH * (j // 2), DH)
                            cos = tab[:, 2 * i, w].unsqueeze(1).to_broadcast([P, HEADS, DH])
                            sin = tab[:, 2 * i + 1, w].rearrange("p (u f) -> p u f", u=2).unsqueeze(1).to_broadcast([P, HEADS, 2, 32])
                            eng.wait_ge(r_evac, G * 6 + 2 + 2 * i + 1)
                            if s is None or s >= 2:
                                eng.wait_ge(qkT_done, g2 * 4 + 2 + 2 * i)
                            eng.tensor_tensor(cosp[:, r, i, :].rearrange("p (h d) -> p h d", d=DH), src, cos, ALU.mult).then_inc(rot_done, 1)
                            if s is None or s >= 1:
                                eng.wait_ge(rot_added, G * 2 - 1 + i + 1)
                            swapped = qk[:, i, :].rearrange("p (h u f) -> p h u f", u=2, f=32)[:, :, ::-1, :]
                            eng.tensor_tensor(sinp[:, i, :].rearrange("p (h u f) -> p h u f", u=2, f=32), swapped, sin, ALU.mult).then_inc(rot_done, 1)
                        for i in range(2):
                            eng.wait_ge(sq_done, G * 2 + 1 + i + 1)
                            if i == 0:
                                eng.wait_ge(norm_step, G * (NSTEPS + 2) + 1)
                            eng.tensor_reduce(ssq[:, HEADS * i:HEADS * i + HEADS], sq[:, i, :].rearrange("p (h d) -> p h d", d=DH),
                                              AX_X, ALU.add).then_inc(ssq_done, 1)
                        base = G * (NSTEPS + 2)
                        eng.wait_ge(ssq_done, G * 2 + 3)
                        eng.tensor_scalar(ssq[:, :], ssq[:, :], 1e-24, None, ALU.max).then_inc(norm_step, 1)
                        eng.wait_ge(norm_step, base + 2)
                        rsqrt(eng, ssq[:, :], rbits[:, :], rhalf[:, :], rtmp[:, :], norm_step, base + 2)
                        eng.wait_ge(norm_step, base + 1 + NSTEPS + 1)
                        if s is None or s >= 1:
                            eng.wait_ge(rot_ready, G * 2 + 1)
                        eng.tensor_copy(rnorm[:, :], rtmp[:, :]).then_inc(norm_step, 1)
                    if active(s, 1):
                        eng.wait_ge(sims_done, g1 + 2)
                        eng.wait_ge(centered, g1 + 1)
                        eng.tensor_reduce(mx[:, :], scores, AX_X, ALU.max).then_inc(max_done, 1)
                        eng.wait_ge(max_done, g1 + 1)
                        eng.wait_ge(exp_done, g1 + 1)
                        eng.tensor_tensor(sh[:, :].rearrange("p (h k) -> p h k", k=DH), scores,
                                          mx[:, :].unsqueeze(2).to_broadcast([P, HEADS, DH]), ALU.subtract).then_inc(centered, 1)

                attention_steps(eng, L, step)
                eng.wait_ge(ffn_in, L * (16 * 13) + 16 * 13)

                def ffn(C, has_a, has_b, has_c, col=None):
                    c1 = C - 1
                    if has_c:
                        c2 = C - 2
                        eng.wait_ge(fy_done, c2 + 2)
                        eng.scalar_tensor_tensor(out=xa[:, :, bass.ds(col, WIN)], in0=ps[:, 5, 0:CH].rearrange("p (b t) -> p b t", b=BATCH),
                                                 scalar=vec[:, 2:3], in1=xb[:, :, bass.ds(col, WIN)], op0=ALU.add, op1=ALU.add).then_inc(x_updated, 1)

                    def glu(m):
                        if has_b:
                            fn = FT[m][1]
                            eng.wait_ge(gelu_done, c1 * 3 + m + 1)
                            if m == 0:
                                eng.wait_ge(fy_done, c1 + 1)
                            eng.scalar_tensor_tensor(out=hh[0:fn, m, :], in0=ps[0:fn, 2 + m, 0:256], scalar=vec[0:fn, 3 + m:4 + m],
                                                     in1=ge[0:fn, m, :], op0=ALU.add, op1=ALU.mult).then_inc(glu_done, 1)

                    if has_a:
                        eng.wait_ge(mean_done, C + 1)
                        eng.wait_ge(xn_done, C + 1)
                        eng.tensor_tensor(cc, xc, ps[:, 0, 0:CH], ALU.subtract).then_inc(ctr_done, 1)
                    glu(0)
                    if has_a:
                        base = C * (NSTEPS + 3)
                        eng.wait_ge(var_done, C + 1)
                        eng.wait_ge(fnorm_step, base + 1)
                        eng.tensor_scalar(fx[:, :], ps[:, 1, 0:2], EPS, None, ALU.add).then_inc(fnorm_step, 1)
                        eng.wait_ge(fnorm_step, base + 2)
                        rsqrt(eng, fx[:, :], fbits[:, :], fhalf[:, :], fr[:, :], fnorm_step, base + 2)
                        eng.wait_ge(fnorm_step, base + 1 + NSTEPS + 1)
                        eng.wait_ge(bc_done, C + 1)
                        for g in range(2):
                            eng.tensor_scalar(dg[:, 128 * g:128 * g + 128], ident[:, :], fr[:, g:g + 1], None, ALU.mult).then_inc(fnorm_step, 1)
                    glu(1)
                    glu(2)
                    if has_a:
                        eng.wait_ge(bc_done, C + 2)
                        eng.wait_ge(ctr_done, C + 2)
                        eng.wait_ge(affine_done, C + 1)
                        eng.tensor_tensor(xn, cc, ps[:, 1, 128:128 + CH], ALU.mult).then_inc(xn_done, 1)

                ffn(L * NW, True, False, False)
                ffn(L * NW + 1, True, True, False)
                with eng.Fori(2, NW) as c:
                    ffn(eng.snap(L * NW + c), True, True, True, c * WIN - (2 * WIN - 1))
                ffn(L * NW + NW, False, True, True, (NW - 2) * WIN + 1)
                ffn(L * NW + NW + 1, False, False, True, (NW - 1) * WIN + 1)
            for b in range(BATCH):
                eng.wait_ge(x_updated, DEPTH * NW + 1)
                eng.wait_ge(end_turned, b + 1)
                eng.tensor_copy(hs.rearrange("p a n -> p (a n)"), xa[:, b, 1:1 + SEQ]).then_inc(end_read, 1)
                eng.wait_ge(end_turned, b + 2)
                if b >= 2:
                    eng.wait_ge((out_done2 if b % 2 else out_done), 16 * (b // 2))
                eng.tensor_tensor(fin[:, b % 2, :, :], ps[:, 0, :].rearrange("p (j d) -> p j d", j=TB), x1[:, b, :, :], ALU.add).then_inc(end_added, 1)


def rotary_tables():
    half = np.arange(0, DH, 2, dtype=np.float32)
    inv = (np.float32(1.0) / np.float32(10000.0) ** (half / np.float32(DH))).astype(np.float32)
    t = np.arange(SEQ, dtype=np.float32)
    f = t[:, None] * inv[None, :]
    f = np.concatenate([f, f], -1)
    base = (half + np.float32(0.4 * DH)) / np.float32(1.4 * DH)
    power = (t - SEQ // 2) / np.float32(WIN // 2)
    sc = (base[None, :] ** power[:, None]).astype(np.float32)
    sc = np.concatenate([sc, sc], -1)
    sign = np.where(np.arange(DH) < DH // 2, -1.0, 1.0).astype(np.float32)
    c, s = np.cos(f), np.sin(f) * sign
    inv_sc = np.float32(1.0) / sc
    full = np.stack([c * sc, s * sc, c * inv_sc, s * inv_sc]).astype(np.float32)
    tile = full.reshape(4, NW, WIN, DH).transpose(2, 0, 1, 3).reshape(WIN, 4, NW * DH)
    return np.ascontiguousarray(np.tile(tile, (GB, 1, 1)))


def mask_table():
    q = np.arange(WIN)[:, None]
    k = np.arange(WIN)[None, :]
    own = np.where(k <= q, 0.0, MASKED)
    before = np.where(k >= q, 0.0, MASKED)
    none = np.full((WIN, WIN), MASKED)
    m = np.stack([np.concatenate(x, 1) for x in ((own, before), (before, own), (own, none))], 1)
    return np.ascontiguousarray(np.tile(m, (GB, 1, 1)).astype(np.float32))


_INS = ["L0_attn_x", "L0_attn_A", "L0_attn_B", "L0_attn_C", "L0_attn_gamma", "L0_attn_beta", "L0_ffn_Wqkv", "L0_ffn_q_scale",
        "L0_ffn_k_scale", "L0_ffn_Wo", "L0_ffn_ln_g", "L0_ffn_ln_b", "L0_ffn_W1", "L0_ffn_b1", "L0_ffn_W2", "L0_ffn_b2"]


def kernel(**inputs):
    import concourse.bacc as bacc
    from concourse.bass_utils import run_bass_kernel_spmd

    nc = bacc.Bacc("TRN2", target_bir_lowering=False, num_devices=1)
    arrays, aps = {}, {}
    data = {n: np.ascontiguousarray(inputs[n]) for n in _INS}
    data.update(tab=rotary_tables(), mask=mask_table(), ident=np.eye(P, dtype=np.float32))
    for name, v in data.items():
        arrays["in_" + name] = v
        aps[name] = nc.dram_tensor("in_" + name, v.shape, mybir.dt.from_np(v.dtype), kind="ExternalInput").ap()
    aps["out"] = nc.dram_tensor("out_0", (BATCH, SEQ, D), F32, kind="ExternalOutput").ap()
    build(nc, aps)
    r = run_bass_kernel_spmd(nc, [arrays], core_ids=[0])
    return r.results[0]["out_0"]
```

```python
from contextlib import ExitStack

import numpy as np

import concourse.bass as bass
from concourse import mybir

ALU = mybir.AluOpType
ACT = mybir.ActivationFunctionType
AX_X = mybir.AxisListType.X
F32 = mybir.dt.float32
BF16 = mybir.dt.bfloat16
I32 = mybir.dt.int32

P = 128
BATCH, SEQ, D = 8, 512, 128
DEPTH, HEADS, DH, WIN = 6, 16, 64, 32
INNER = HEADS * DH
FF = int(D * 4 * 2 / 3)
FT = [(0, 128), (128, 128), (256, FF - 256)]
NW = SEQ // WIN
FW = 64
NC = SEQ // FW
CH = BATCH * FW
GB = P // WIN
NG = BATCH // GB
TILES = NW * NG
HP = HEADS // 2
ROUND = 4
TURNS = TILES // ROUND
BLK = 64
NBLK = SEQ // BLK
TB = SEQ // P
EPS = 1e-5
MASKED = -1e30
MAGIC = 0x5F3759DF
NEWTON = 3
NSTEPS = 2 + 3 * NEWTON
SCALE = 8.0
SEED_OPS = 2


def rsqrt(eng, x, bits, half, y, sem, base):
    eng.tensor_scalar(bits, x.bitcast(I32), 1, None, ALU.logical_shift_right).then_inc(sem, 1)
    eng.wait_ge(sem, base + 1)
    eng.tensor_scalar(y.bitcast(I32), bits, -1, MAGIC, ALU.mult, ALU.add).then_inc(sem, 1)
    n = 2
    for _ in range(NEWTON):
        eng.wait_ge(sem, base + n)
        eng.tensor_tensor(half, y, y, ALU.mult).then_inc(sem, 1)
        eng.wait_ge(sem, base + n + 1)
        eng.scalar_tensor_tensor(out=half, in0=half, scalar=-0.5, in1=x, op0=ALU.mult, op1=ALU.mult).then_inc(sem, 1)
        eng.wait_ge(sem, base + n + 2)
        eng.scalar_tensor_tensor(out=y, in0=half, scalar=1.5, in1=y, op0=ALU.add, op1=ALU.mult).then_inc(sem, 1)
        n += 3



class Steps:

    def __init__(self, eng, sem, base):
        self.eng, self.sem, self.base, self.n = eng, sem, base, 0

    def __call__(self, ins):
        ins.then_inc(self.sem, 1)
        self.n += 1
        self.eng.wait_ge(self.sem, self.base + self.n)


def layernorm(eng, step, src, dst, c, t4, bits):
    shape = [P, TB, D]
    mean, var, half, r = (t4[:, i, :] for i in range(4))
    step(eng.tensor_reduce(mean, src, AX_X, ALU.add))
    step(eng.tensor_scalar(mean, mean, 1.0 / D, None, ALU.mult))
    step(eng.tensor_tensor(dst, src, mean.unsqueeze(2).to_broadcast(shape), ALU.subtract))
    step(eng.tensor_tensor(c, dst, dst, ALU.mult))
    step(eng.tensor_reduce(var, c, AX_X, ALU.add))
    step(eng.tensor_scalar(var, var, 1.0 / D, EPS, ALU.mult, ALU.add))
    rsqrt(eng, var, bits, half, r, step.sem, step.base + step.n)
    step.n += NSTEPS
    eng.wait_ge(step.sem, step.base + step.n)
    step(eng.tensor_tensor(dst, dst, r.unsqueeze(2).to_broadcast(shape), ALU.mult))


LN_STEPS = 7 + NSTEPS
POST_STEPS = 2 + LN_STEPS + 3 + LN_STEPS
DMA_V = 2 * GB


def build(nc, a):
    with ExitStack() as ctx:
        def sb(name, shape, dt=F32):
            return ctx.enter_context(nc.sbuf_tensor(name, shape, dt))

        def sem(name):
            return ctx.enter_context(nc.semaphore(name))

        ident = sb("ident", [P, P])
        ident_bf = sb("ident_bf", [P, P], BF16)
        ones = sb("ones", [P, P])
        mean_w = sb("mean_w", [P, P])
        mask_f = sb("mask_f", [P, 3, DH])
        mask = sb("mask", [P, 3, DH], BF16)
        x1 = sb("x1", [P, BATCH, TB, D])
        xa = sb("xa", [P, BATCH, 1 + SEQ])
        xb = sb("xb", [P, BATCH, 1 + SEQ])
        w_qkv = sb("w_qkv", [P, 3, INNER])
        w_o = sb("w_o", [P, HP, D])
        w_1 = sb("w_1", [P, 2 * FF])
        w_2 = sb("w_2", [P, 3, D])
        tab = sb("tab", [P, 4, NW * DH])
        qks = sb("qks", [P, 4, DH])
        vec = sb("vec", [P, 9])
        xs = sb("xs", [P, 2, P])
        qk = sb("qk", [P, 2, INNER])
        cosp = sb("cosp", [P, 2, 2, INNER])
        sinp = sb("sinp", [P, 2, INNER])
        sq = sb("sq", [P, 2, INNER])
        ssq = sb("ssq", [P, 2 * HEADS])
        rbits = sb("rbits", [P, 2 * HEADS], I32)
        rhalf = sb("rhalf", [P, 2 * HEADS])
        rtmp = sb("rtmp", [P, 2 * HEADS])
        rnorm = sb("rnorm", [P, 2 * HEADS])
        qT = sb("qT", [P, HP, P])
        kT = sb("kT", [P, NG, HP, GB, 2 * WIN])
        sh = sb("sh", [P, INNER])
        ex = sb("ex", [P, INNER])
        mx = sb("mx", [P, HEADS])
        esum = sb("esum", [P, HEADS])
        rsum = sb("rsum", [P, HEADS])
        aT = sb("aT", [P, 8, P])
        vt = sb("vt", [P, 2, 2, 512])
        vk = sb("vk", [P, NG, GB, 512])
        on = sb("on", [P, INNER])
        oT = sb("oT", [P, HP, P])
        room = cosp.rearrange("p a b n -> p (a b n)")
        xc, cc, cq, xn, xf, dg = (room[:, i * CH:(i + 1) * CH] for i in range(6))
        hh = sinp.rearrange("p a n -> p (a n)")[:, 0:3 * CH].rearrange("p (m n) -> p m n", m=3)
        ge = sq.rearrange("p a n -> p (a n)")[:, 0:3 * CH].rearrange("p (m n) -> p m n", m=3)
        fx = sb("fx", [P, CH // P])
        fbits = sb("fbits", [P, CH // P], I32)
        fhalf = sb("fhalf", [P, CH // P])
        fr = sb("fr", [P, CH // P])
        xnt = tab.rearrange("p a (b n) -> p (a b) n", b=2).rearrange("p b (j d) -> p b j d", j=TB)
        xnf = kT.rearrange("p g h b k -> p (g h b k)").rearrange("p (b t) -> p b t", b=BATCH)
        hall = vk.rearrange("p g b n -> p (g b) n")
        hb = cosp.rearrange("p a b n -> p (a b n)")[:, 0:2 * BLK * BATCH].rearrange("p (r t b) -> p r t b", r=2, b=BATCH)
        lnc = sq.rearrange("p a n -> p (a n)")[:, 0:512].rearrange("p (j d) -> p j d", j=TB)
        lnd = sinp.rearrange("p a n -> p (a n)")[:, 0:512].rearrange("p (j d) -> p j d", j=TB)
        lno = on[:, 0:512].rearrange("p (j d) -> p j d", j=TB)
        hs = oT[:, 0:TB, :]
        abc = qT[:, 0:3, :]
        abcT = qT[:, 3:6, :]
        gam = aT[:, 0, :]
        bet = aT[:, 1, :]
        t4 = sb("t4", [P, 4, TB])
        b4 = sb("b4", [P, TB], I32)
        fin = sb("fin", [P, 2, TB, D])
        ps = ctx.enter_context(nc.psum_tensor("ps", [P, 8, 512], F32))

        consts_in = sem("consts_in")
        x_in = sem("x_in")
        zeroed = sem("zeroed")
        abc_in = sem("abc_in")
        abc_turned = sem("abc_turned")
        abc_out = sem("abc_out")
        ln1_step = sem("ln1_step")
        ln1_turned = sem("ln1_turned")
        ln1_out = sem("ln1_out")
        pre_done = sem("pre_done")
        h_done = sem("h_done")
        hall_done = sem("hall_done")
        post_step = sem("post_step")
        hs_turned = sem("hs_turned")
        post_turned = sem("post_turned")
        xa_out = sem("xa_out")
        qkv_in = sem("qkv_in")
        tables_in = sem("tables_in")
        tables_ready = sem("tables_ready")
        wo_in = sem("wo_in")
        ffn_in = sem("ffn_in")
        xs_ready = sem("xs_ready")
        proj_done = sem("proj_done")
        r_evac = sem("r_evac")
        rot_done = sem("rot_done")
        sq_done = sem("sq_done")
        ssq_done = sem("ssq_done")
        norm_step = sem("norm_step")
        rot_added = sem("rot_added")
        rot_ready = sem("rot_ready")
        qkT_done = sem("qkT_done")
        qk_evac = sem("qk_evac")
        sims_done = sem("sims_done")
        max_done = sem("max_done")
        centered = sem("centered")
        exp_done = sem("exp_done")
        rsum_done = sem("rsum_done")
        recip_done = sem("recip_done")
        aT_done = sem("aT_done")
        at_evac = sem("at_evac")
        pv_done = sem("pv_done")
        o_read = sem("o_read")
        oT_done = sem("oT_done")
        ot_evac = sem("ot_evac")
        y_done = sem("y_done")
        y_added = sem("y_added")
        xc_ready = sem("xc_ready")
        mean_done = sem("mean_done")
        ctr_done = sem("ctr_done")
        csq_done = sem("csq_done")
        var_done = sem("var_done")
        fnorm_step = sem("fnorm_step")
        bc_done = sem("bc_done")
        xn_done = sem("xn_done")
        affine_done = sem("affine_done")
        hg_done = sem("hg_done")
        gelu_done = sem("gelu_done")
        glu_done = sem("glu_done")
        fy_done = sem("fy_done")
        x_updated = sem("x_updated")
        end_read = sem("end_read")
        end_turned = sem("end_turned")
        end_added = sem("end_added")
        out_done = sem("out_done")
        out_done2 = sem("out_done2")
        mask_in = sem("mask_in")

        from_one = (
            r_evac, proj_done, rot_done, y_done, y_added, x_updated, ssq_done, sq_done, norm_step, sims_done,
            centered, exp_done, rsum_done, recip_done, aT_done, pv_done, o_read, oT_done, glu_done, xn_done,
            ctr_done, fy_done, fnorm_step, bc_done, affine_done, h_done, hall_done, ln1_step, post_step,
            ln1_out, post_turned, xa_out, end_added, end_turned, at_evac, rot_added, rot_ready, qk_evac,
            ot_evac,
        )

        def settled(eng):
            eng.sem_inc(carried[eng.engine.name], 1)

        carried = {n: sem("carried_" + n) for n in ("PE", "DVE", "Activation", "Pool")}
        v_landed = [sem(f"v_landed{i}") for i in range(ROUND)]
        block = ctx.enter_context(nc.Block())

        R = lambda n: ps[:, n % 2, :]
        T = lambda n: ps[:, 2 + n % 2, :]
        scores = ps[:, 4:6, :].rearrange("p a (h k) -> p (a h) k", k=DH)
        O = lambda x: ps[:, 6 + x, :]

        def attention_steps(eng, L, step, head=0):
            steps = TILES + 3
            for s in range(ROUND):
                step(s, L * TILES + s, L * TURNS, s)
            with eng.Fori(1, TURNS) as it:
                g0 = eng.snap(L * TILES + it * ROUND)
                q0 = eng.snap(L * TURNS + it)
                for j in range(ROUND):
                    step(j, g0 + j, q0, None, it)
            for s in range(TILES, steps):
                step(s % ROUND, L * TILES + s, L * TURNS + TURNS, s)

        def active(s, back):
            return s is None or 0 <= s - back < TILES

        @block.sync
        def _(eng):
            for name, dst in (("ident", ident[:, :]), ("mask", mask_f[:, :, :])):
                eng.dma_start(dst, a[name]).then_inc(consts_in, 16)
            for i, name in enumerate("ABC"):
                eng.dma_start(abc[:, i, :], a["L0_attn_" + name]).then_inc(abc_in, 16)
            for name, dst in (("L0_attn_gamma", gam), ("L0_attn_beta", bet)):
                eng.dma_start(dst, a[name].rearrange("(o d) -> o d", o=1).to_broadcast([P, D])).then_inc(abc_in, 16)
            for b in range(BATCH):
                eng.dma_start(x1[:, b, :, :], a["L0_attn_x"][b].rearrange("(j p) d -> p j d", p=P)).then_inc(x_in, 16)
            for signal in from_one:
                eng.sem_inc(signal, 1)
            with eng.Fori(0, DEPTH) as L:
                eng.wait_ge(proj_done, L * (6 * TILES) + 1)
                eng.dma_start(w_qkv[:, :, :].rearrange("p a n -> p (a n)"),
                              a["L0_ffn_Wqkv"][bass.ds(L, 1), :, :].rearrange("o p n -> (o p) n")).then_inc(qkv_in, 16)
                eng.wait_ge(rot_done, L * (4 * TILES) + 1)
                eng.wait_ge(post_step, POST_STEPS * BATCH + 1)
                eng.dma_start(tab[:, :, :], a["tab"]).then_inc(tables_in, 16)
                for i, name in ((0, "q"), (2, "k")):
                    src = a[f"L0_ffn_{name}_scale"][bass.ds(L, 1), :]
                    eng.dma_start(qks[:, i, :], src.to_broadcast([P, DH])).then_inc(tables_in, 16)
                    for u in range(2):
                        half = a[f"L0_ffn_{name}_scale"][bass.ds(L, 1), 32 * (1 - u):32 * (1 - u) + 32]
                        eng.dma_start(qks[:, i + 1, 32 * u:32 * u + 32], half.to_broadcast([P, 32])).then_inc(tables_in, 16)
                eng.wait_ge(y_done, L * TILES + 1)
                eng.dma_start(w_o[:, :, :], a["L0_ffn_Wo"][bass.ds(L, 1), :, :].rearrange("o (k p) n -> p (o k) n", p=P)).then_inc(wo_in, 16)
                eng.wait_ge(x_updated, L * NC + 1)
                eng.dma_start(w_1[:, :], a["L0_ffn_W1"][bass.ds(L, 1), :, :].rearrange("o p n -> (o p) n")).then_inc(ffn_in, 16)
                for m, (f0, fn) in enumerate(FT):
                    eng.dma_start(w_2[0:fn, m, :], a["L0_ffn_W2"][bass.ds(L, 1), f0:f0 + fn, :].rearrange("o p n -> (o p) n")).then_inc(ffn_in, 16)
                for i, name in enumerate(("ln_g", "ln_b", "b2")):
                    eng.dma_start(vec[:, i:i + 1], a["L0_ffn_" + name][bass.ds(L, 1), :].rearrange("o p -> p o")).then_inc(ffn_in, 16)
                for u in range(2):
                    for m, (f0, fn) in enumerate(FT):
                        eng.dma_start(vec[0:fn, 3 + 3 * u + m:4 + 3 * u + m],
                                      a["L0_ffn_b1"][bass.ds(L, 1), u * FF + f0:u * FF + f0 + fn].rearrange("o p -> p o")).then_inc(ffn_in, 16)

                def step(j, G, Q, s, it=None):
                    if not active(s, 0):
                        return
                    g, slot = j % 2, j // 2
                    eng.wait_ge(r_evac, G * 6 + 7)
                    if s is None or s >= 2:
                        eng.wait_ge(pv_done, G)
                    for x in range(2):
                        for b in range(GB):
                            eng.dma_start(vk[64 * x + 32 * slot:64 * x + 32 * slot + 32, g, b, :],
                                          vt[32 * b:32 * b + 32, j % 2, x, :]).then_inc(v_landed[j], 16)

                attention_steps(eng, L, step)
            for b in range(BATCH):
                eng.wait_ge(end_added, b + 2)
                eng.dma_start(a["out"][b].rearrange("(j p) d -> p j d", p=P), fin[:, b % 2, :, :]).then_inc((out_done2 if b % 2 else out_done), 16)
            eng.wait_ge(out_done, 16 * BATCH // 2)
            eng.wait_ge(out_done2, 16 * BATCH // 2)

        @block.gpsimd
        def _(eng):
            eng.memset(ones[:, :], 1.0).then_inc(zeroed, 1)
            eng.memset(mean_w[:, :], 1.0 / D).then_inc(zeroed, 1)
            eng.memset(xa[:, :, 0:1], 0.0).then_inc(zeroed, 1)
            eng.memset(xb[:, :, 0:1], 0.0).then_inc(zeroed, 1)
            eng.memset(hb[:, 1, BLK - 1, :], 0.0).then_inc(zeroed, 1)
            with eng.Fori(0, NBLK // 2) as it:
                for r in range(2):
                    eng.wait_ge(h_done, it * (2 * BLK) + (r + 1) * BLK + 1)
                    eng.tensor_copy(hall[:, :, bass.ds(it * (2 * BLK) + r * BLK, BLK)],
                                    hb[:, r, :, :].rearrange("p t b -> p b t")).then_inc(hall_done, 1)
            with eng.Fori(0, DEPTH) as L:
                eng.wait_ge(tables_in, L * (16 * 7) + 16 * 7)
                for i in range(4):
                    t = tab[:, i, :].rearrange("p (w d) -> p w d", d=DH)
                    eng.tensor_tensor(t, t, qks[:, i, :].unsqueeze(1).to_broadcast([P, NW, DH]), ALU.mult).then_inc(tables_ready, 1)
                def step(j, G, Q, s, it=None):
                    if active(s, 1):
                        r, g1 = (j - 1) % 2, G - 1
                        for i in range(2):
                            eng.wait_ge(rot_done, g1 * 4 + 2 * i + 3)
                            eng.tensor_tensor(cosp[:, r, i, :], cosp[:, r, i, :], sinp[:, i, :], ALU.add).then_inc(rot_added, 1)
                        eng.wait_ge(norm_step, g1 * (NSTEPS + 2) + NSTEPS + 3)
                        for i in range(2):
                            eng.wait_ge(rot_added, g1 * 2 + i + 2)
                            v = cosp[:, r, i, :].rearrange("p (h d) -> p h d", d=DH)
                            eng.tensor_tensor(v, v, rnorm[:, HEADS * i:HEADS * i + HEADS].unsqueeze(2).to_broadcast([P, HEADS, DH]),
                                              ALU.mult).then_inc(rot_ready, 1)

                attention_steps(eng, L, step)


        @block.tensor
        def _(eng):
            eng.wait_ge(abc_in, 16 * 5)
            eng.wait_ge(consts_in, 32)
            for i in range(3):
                eng.transpose(ps[:, 0, 128 * i:128 * i + 128], abc[:, i, :], ident[:, :]).then_inc(abc_turned, 1)
            with eng.Fori(0, BATCH) as b:
                eng.wait_ge(ln1_step, b * LN_STEPS + LN_STEPS + 1)
                eng.wait_ge(ln1_out, b * 2 + 1)
                for j in range(TB):
                    t = eng.transpose(ps[:, 1, 128 * j:128 * j + 128], lnd[:, j, :], ident[:, :])
                t.then_inc(ln1_turned, 1)
            eng.wait_ge(ln1_out, 2 * BATCH + 1)
            eng.wait_ge(abc_out, 1)
            eng.wait_ge(zeroed, 5)
            with eng.Fori(0, NBLK // 2) as it:
                for r in range(2):
                    h0 = it * (2 * BLK) + r * BLK
                    eng.wait_ge(h_done, h0 + 1)
                    settled(eng)
                    eng.matmul(ps[:, r, :], abcT[:, 1, :], xnf[:, :, bass.ds(h0, BLK)].rearrange("p b t -> p t b"),
                               start=True, stop=False, skip_group_check=True)
                    for t in range(BLK):
                        if t:
                            eng.wait_ge(h_done, h0 + t + 1)
                        prev = hb[:, r, t - 1, :] if t else hb[:, 1 - r, BLK - 1, :]
                        eng.matmul(ps[:, r, BATCH * t:BATCH * t + BATCH], abcT[:, 0, :], prev, start=False, stop=t == BLK - 1,
                                   skip_group_check=True).then_inc(pre_done, 1)
            with eng.Fori(0, BATCH) as b:
                eng.wait_ge(post_step, b * POST_STEPS + 2)
                for j in range(TB):
                    t = eng.matmul(ps[:, 2, 128 * j:128 * j + 128], hs[:, j, :], abcT[:, 2, :], start=True, stop=True)
                t.then_inc(hs_turned, 1)
                eng.wait_ge(post_step, b * POST_STEPS + POST_STEPS + 1)
                eng.wait_ge(xa_out, b + 1)
                for j in range(TB):
                    t = eng.transpose(ps[:, 3, 128 * j:128 * j + 128], lnd[:, j, :], ident[:, :])
                t.then_inc(post_turned, 1)
            with eng.Fori(0, DEPTH) as L:
                eng.wait_ge(qkv_in, L * 16 + 16)
                eng.wait_ge(x_updated, L * NC + 1)
                eng.wait_ge(xa_out, BATCH + 1)

                def step(j, G, Q, s, it=None):
                    g1, g2, g3 = (G - 1), (G - 2), (G - 3)
                    gg, slot = (j - 1) % 2, ((j - 1) % ROUND) // 2

                    def project(c):
                        if c == 0:
                            eng.wait_ge(xs_ready, G * 2 + 2)
                            eng.wait_ge(r_evac, G * 6 + 1)
                        if c == 1 and (s is None or s >= 4):
                            eng.wait_ge(y_added, G - 2)
                        if c >= 2:
                            eng.wait_ge(r_evac, G * 6 + c)
                        if c < 4:
                            w = w_qkv[:, c // 2, 512 * (c % 2):512 * (c % 2) + 512]
                        else:
                            w = w_qkv[:, 2, :].rearrange("p (m x h d) -> p x h m d", m=4, x=2, h=2)[:, c % 2]
                        eng.matmul(R(7 * j + c), xs[:, j % 2, :], w, start=True, stop=True).then_inc(proj_done, 1)

                    def turn_rotated(i):
                        eng.wait_ge(rot_ready, g1 * 2 + 2 + i)
                        for u in range(2):
                            if i:
                                eng.wait_ge(qk_evac, g1 * 4 + 2 + u)
                            elif active(s, 3):
                                eng.wait_ge(ot_evac, g3 * 2 + 2 + u)
                            elif s == 2:
                                eng.wait_ge(qk_evac, g1 * 4 + u)
                            for k in range(4):
                                hp = 4 * u + k
                                t = eng.transpose(T(u)[:, 128 * k:128 * k + 128], cosp[:, (j - 1) % 2, i, 128 * hp:128 * hp + 128], ident[:, :])
                            t.then_inc(qkT_done, 1)

                    if active(s, 0):
                        for c in range(3):
                            project(c)
                    if active(s, 3):
                        eng.wait_ge(o_read, g3 * 2 + 3)
                        for u in range(2):
                            eng.wait_ge(at_evac, g3 * 2 + 2 + u)
                            for k in range(4):
                                t = eng.transpose(T(u)[:, 128 * k:128 * k + 128], on[:, 512 * u + 128 * k:512 * u + 128 * k + 128], ident[:, :])
                            t.then_inc(oT_done, 1)
                    if active(s, 0):
                        for c in range(3, 6):
                            project(c)
                    if active(s, 1):
                        turn_rotated(0)
                    if active(s, 3):
                        if active(s, 0):
                            eng.wait_ge(r_evac, G * 6 + 6)
                        else:
                            eng.wait_ge(r_evac, L * (6 * TILES) + 6 * TILES + 1)
                            eng.wait_ge(y_added, g3 + 1)
                        if s == 3:
                            eng.wait_ge(wo_in, L * 16 + 16)
                        eng.wait_ge(ot_evac, g3 * 2 + 3)
                        for k in range(HP):
                            t = eng.matmul(R(7 * j + 6)[:, 0:P], w_o[:, k, :], oT[:, k, :], start=k == 0, stop=k == HP - 1)
                        t.then_inc(y_done, 1)
                    if active(s, 1):
                        turn_rotated(1)
                        eng.wait_ge(mask_in, 2)
                        eng.wait_ge(centered, g1 + 1)
                        variant = 2 if s is not None and s - 1 < 2 else slot
                        for h2 in range(2):
                            eng.matmul(ps[:, 4 + h2, :].rearrange("p (h k) -> p h k", k=DH), ident_bf[:, :],
                                       mask[:, variant, :].unsqueeze(1).to_broadcast([P, 8, DH]), start=True, stop=False, skip_group_check=True)
                    if active(s, 2):
                        eng.wait_ge(exp_done, g2 + 2)
                        for u in range(2):
                            if active(s, 1):
                                eng.wait_ge(qk_evac, g1 * 4 + 4 + u)
                            else:
                                eng.wait_ge(ot_evac, g3 * 2 + 2 + u)
                            for k in range(4):
                                t = eng.transpose(T(u)[:, 128 * k:128 * k + 128], ex[:, 512 * u + 128 * k:512 * u + 128 * k + 128], ident[:, :])
                            t.then_inc(aT_done, 1)
                    if active(s, 1):
                        eng.wait_ge(qk_evac, g1 * 4 + 5)
                        settled(eng)
                        for h2 in range(2):
                            rows = slice(64 * h2, 64 * h2 + 64)
                            for hp in range(HP):
                                for b in range(GB):
                                    t = eng.matmul(ps[32 * b:32 * b + 32, 4 + h2, DH * hp:DH * hp + DH], qT[rows, hp, 32 * b:32 * b + 32],
                                                   kT[rows, gg, hp, b, :], start=False, stop=hp == HP - 1, skip_group_check=True)
                        t.then_inc(sims_done, 1)
                    if active(s, 2):
                        eng.wait_ge(at_evac, g2 * 2 + 3)
                        eng.wait_ge(o_read, g2 * 2 + 1)
                        eng.wait_ge(v_landed[(j - 2) % ROUND], (Q + ((j - 2) // ROUND + 1)) * (16 * DMA_V))
                        settled(eng)
                        for x in range(2):
                            rows = slice(64 * x, 64 * x + 64)
                            for k in range(8):
                                for b in range(GB):
                                    t = eng.matmul(ps[32 * b:32 * b + 32, 6 + x, DH * k:DH * k + DH], aT[rows, k, 32 * b:32 * b + 32],
                                                   vk[rows, j % 2, b, DH * k:DH * k + DH], start=True, stop=True)
                        t.then_inc(pv_done, 1)

                attention_steps(eng, L, step)

                eng.wait_ge(y_added, L * TILES + TILES + 1)
                eng.wait_ge(ffn_in, L * (16 * 13) + 16 * 13)

                def ffn(C, has_a, has_b, has_c, first_b=False):
                    c1, c2 = C - 1, C - 2
                    if has_c:
                        eng.wait_ge(glu_done, c2 * 3 + 4)
                        eng.wait_ge(x_updated, c2 + 1)
                        for m, (f0, fn) in enumerate(FT):
                            t = eng.matmul(ps[:, 6, :], w_2[0:fn, m, :], hh[0:fn, m, :], start=m == 0, stop=m == 2)
                        t.then_inc(fy_done, 1)
                    if has_a:
                        eng.wait_ge(xc_ready, C * 2 + 2)
                        eng.wait_ge(ctr_done, C + 1)
                        eng.matmul(ps[:, 0, :], mean_w[:, :], xc, start=True, stop=True).then_inc(mean_done, 1)

                    def w1(m):
                        f0, fn = FT[m]
                        if m == 0:
                            eng.wait_ge(affine_done, c1 + 2)
                        if m != 1 or not first_b:
                            eng.wait_ge(glu_done, c1 * 3 + (1, 0, 2)[m])
                        for u in (1, 0):
                            t = eng.matmul(ps[0:fn, 2 + 2 * (m % 2) + u, :], w_1[:, u * FF + f0:u * FF + f0 + fn], xf, start=True, stop=True)
                        t.then_inc(hg_done, 1)

                    if has_b:
                        w1(0)
                    if has_a:
                        eng.wait_ge(csq_done, C + 1)
                        for g in range(CH // P):
                            t = eng.matmul(ps[:, 7, g:g + 1], cq[:, P * g:P * g + P], mean_w[:, 0:1], start=True, stop=True)
                        t.then_inc(var_done, 1)
                    if has_b:
                        w1(1)
                        w1(2)
                    if has_a:
                        eng.wait_ge(fnorm_step, C * (NSTEPS + 2) + NSTEPS + 3)
                        eng.wait_ge(xn_done, C + 1)
                        eng.matmul(ps[:, 1, :], ones[:, :], dg, start=True, stop=True).then_inc(bc_done, 1)

                ffn(L * NC, True, False, False)
                ffn(L * NC + 1, True, True, False, True)
                with eng.Fori(2, NC) as c:
                    ffn(eng.snap(L * NC + c), True, True, True)
                ffn(L * NC + NC, False, True, True)
                ffn(L * NC + NC + 1, False, False, True)
            with eng.Fori(0, BATCH) as b:
                eng.wait_ge(end_read, b + 1)
                eng.wait_ge(end_added, b + 1)
                for j in range(TB):
                    t = eng.transpose(ps[:, 0, 128 * j:128 * j + 128], hs[:, j, :], ident[:, :])
                t.then_inc(end_turned, 1)

        @block.scalar
        def _(eng):
            eng.wait_ge(abc_turned, 3)
            eng.copy(abcT.rearrange("p a n -> p (a n)"), ps[:, 0, 0:384]).then_inc(abc_out, 1)
            with eng.Fori(0, BATCH) as b:
                eng.wait_ge(ln1_step, b * LN_STEPS + LN_STEPS + 1)
                eng.copy(xnt[:, bass.ds(b, 1), :, :].rearrange("p o j d -> p (o j) d"), lnd).then_inc(ln1_out, 1)
                eng.wait_ge(ln1_turned, b + 1)
                eng.copy(xnf[:, bass.ds(b, 1), :].rearrange("p o t -> p (o t)"), ps[:, 1, :]).then_inc(ln1_out, 1)
            with eng.Fori(0, NBLK // 2) as it:
                for r in range(2):
                    h0 = it * (2 * BLK) + r * BLK
                    for t in range(BLK):
                        eng.wait_ge(pre_done, h0 + t + 1)
                        if t == 0:
                            eng.wait_ge(hall_done, (it * 2 + r - 1 if r else it * 2) + 1)
                        eng.activation(hb[:, r, t, :], ps[:, r, BATCH * t:BATCH * t + BATCH], ACT.Tanh).then_inc(h_done, 1)
            with eng.Fori(0, BATCH) as b:
                eng.wait_ge(post_turned, b + 2)
                eng.copy(xa[:, bass.ds(b, 1), 1:1 + SEQ].rearrange("p o t -> p (o t)"), ps[:, 3, :]).then_inc(xa_out, 1)
            with eng.Fori(0, DEPTH) as L:
                eng.wait_ge(x_updated, L * NC + 1)

                def shifted(dst, src, batches, col, signal, steps=WIN):
                    for h in range(2):
                        rows = slice(64 * h, 64 * h + 64)
                        cols = slice(col + 1 - h, col + 1 - h + steps) if isinstance(col, int) else bass.ds(col + (1 - h), steps)
                        eng.copy(dst[rows], src[rows, batches, cols]).then_inc(signal, 1)

                def step(j, G, Q, s, it=None):
                    g1, g2, g3 = (G - 1), (G - 2), (G - 3)
                    if active(s, 0):
                        if s is None or s >= 2:
                            eng.wait_ge(proj_done, G * 6 - 5)
                        col = 32 * (s // 2) if s is not None else it * (2 * WIN) + 32 * (j // 2)
                        settled(eng)
                        shifted(xs[:, j % 2, :].rearrange("p (b t) -> p b t", b=GB), xa, slice(GB * (j % 2), GB * (j % 2) + GB), col, xs_ready)

                    def take(c):
                        if c == 0:
                            eng.wait_ge(sq_done, G * 2 + 1)
                        if c in (0, 2):
                            eng.wait_ge(rot_done, L * (4 * TILES) + 1 if s == 0 else G * 4 - 1 + c)
                        if c == 4 and (s is None or s >= 2):
                            eng.wait_ge(v_landed[(j - 2) % ROUND], (Q + ((j - 2) // ROUND + 1)) * (16 * DMA_V))
                        eng.wait_ge(proj_done, G * 6 + c + 2)
                        dst = qk[:, c // 2, 512 * (c % 2):512 * (c % 2) + 512] if c < 4 else vt[:, j % 2, c % 2, :]
                        eng.copy(dst, R(7 * j + c)).then_inc(r_evac, 1)

                    if active(s, 0):
                        for c in range(3):
                            take(c)
                    if active(s, 3):
                        eng.wait_ge(y_done, g3 + 1)
                        for u in range(2):
                            eng.wait_ge(oT_done, g3 * 2 + 2 + u)
                            eng.copy(oT[:, 4 * u:4 * u + 4, :].rearrange("p a n -> p (a n)"), T(u)).then_inc(ot_evac, 1)
                    if active(s, 0):
                        for c in range(3, 6):
                            take(c)
                    if active(s, 1):
                        eng.wait_ge(sims_done, g1 + 1)
                        for u in range(2):
                            eng.wait_ge(qkT_done, g1 * 4 + 1 + u)
                            eng.copy(qT[:, 4 * u:4 * u + 4, :].rearrange("p a n -> p (a n)"), T(u)).then_inc(qk_evac, 1)
                    if active(s, 2):
                        eng.wait_ge(centered, g2 + 2)
                        eng.wait_ge(rsum_done, g2 + 1)
                        eng.wait_ge(aT_done, g2 * 2 + 1)
                        eng.activation(ex[:, :], sh[:, :], ACT.Exp, scale=SCALE).then_inc(exp_done, 1)
                    if active(s, 1):
                        gg, slot = (j - 1) % 2, ((j - 1) % ROUND) // 2
                        for u in range(2):
                            eng.wait_ge(qkT_done, g1 * 4 + 3 + u)
                            dst = kT[:, gg, 4 * u:4 * u + 4, :, 32 * slot:32 * slot + 32]
                            eng.copy(dst, T(u).rearrange("p (h b t) -> p h b t", h=4, b=GB)).then_inc(qk_evac, 1)
                    if active(s, 2):
                        eng.wait_ge(pv_done, g2 + 1)
                        for u in range(2):
                            eng.wait_ge(aT_done, g2 * 2 + 2 + u)
                            eng.copy(aT[:, 4 * u:4 * u + 4, :].rearrange("p a n -> p (a n)"), T(u)).then_inc(at_evac, 1)
                    if active(s, 0):
                        for i in range(2):
                            eng.wait_ge(ssq_done, L * (2 * TILES) + 1 if s == 0 and i == 0 else G * 2 + i)
                            eng.wait_ge(r_evac, G * 6 + 3 + 2 * i)
                            eng.activation(sq[:, i, :], qk[:, i, :], ACT.Square).then_inc(sq_done, 1)

                attention_steps(eng, L, step)
                eng.wait_ge(ffn_in, L * (16 * 13) + 16 * 13)

                def ffn(C, has_a, has_b, col=None, first_b=False):
                    c1 = C - 1
                    if has_a:
                        eng.wait_ge(y_added, L * TILES + TILES + 1)
                        eng.wait_ge(ctr_done, C + 1)
                        settled(eng)
                        shifted(xc.rearrange("p (b t) -> p b t", b=BATCH), xb, slice(0, BATCH), col, xc_ready, FW)
                        eng.wait_ge(ctr_done, C + 2)
                        eng.activation(cq, cc, ACT.Square).then_inc(csq_done, 1)
                    if has_b:
                        for m, (f0, fn) in enumerate(FT):
                            eng.wait_ge(hg_done, c1 * 3 + m + 1)
                            if not first_b:
                                eng.wait_ge(glu_done, c1 * 3 - 1 + m)
                            eng.activation(ge[0:fn, m, :], ps[0:fn, 3 + 2 * (m % 2), :], ACT.Gelu, bias=vec[0:fn, 6 + m:7 + m]).then_inc(gelu_done, 1)
                    if has_a:
                        eng.wait_ge(xn_done, C + 2)
                        eng.activation(xf, xn, ACT.Identity, bias=vec[:, 1:2], scale=vec[:, 0:1]).then_inc(affine_done, 1)

                ffn(L * NC, True, False, 0)
                ffn(L * NC + 1, True, True, FW, True)
                with eng.Fori(2, NC) as c:
                    ffn(eng.snap(L * NC + c), True, True, c * FW)
                ffn(L * NC + NC, False, True)

        @block.vector
        def _(eng):
            eng.wait_ge(consts_in, 32)
            eng.tensor_copy(ident_bf[:, :], ident[:, :]).then_inc(mask_in, 1)
            eng.tensor_copy(mask[:, :, :], mask_f[:, :, :]).then_inc(mask_in, 1)
            eng.wait_ge(x_in, 16 * BATCH)
            with eng.Fori(0, BATCH) as b:
                eng.wait_ge(ln1_out, b * 2 + 1)
                settled(eng)
                step = Steps(eng, ln1_step, b * LN_STEPS + 1)
                layernorm(eng, step, x1[:, bass.ds(b, 1), :, :].rearrange("p o j d -> p (o j) d"), lnd, lnc, t4, b4[:, :])
                assert step.n == LN_STEPS
            eng.wait_ge(hall_done, NBLK + 1)
            eng.wait_ge(abc_in, 16 * 5)
            with eng.Fori(0, BATCH) as b:
                row = x1[:, bass.ds(b, 1), :, :].rearrange("p o j d -> p (o j) d")
                step = Steps(eng, post_step, b * POST_STEPS + 1)
                eng.wait_ge(post_turned, b + 1)
                step(eng.tensor_copy(hs.rearrange("p a n -> p (a n)"), hall[:, bass.ds(b, 1), :].rearrange("p o t -> p (o t)")))
                eng.wait_ge(hs_turned, b + 1)
                step(eng.tensor_tensor(lno, ps[:, 2, :].rearrange("p (j d) -> p j d", j=TB),
                                       xnt[:, bass.ds(b, 1), :, :].rearrange("p o j d -> p (o j) d"), ALU.add))
                layernorm(eng, step, lno, lnd, lnc, t4, b4[:, :])
                step(eng.tensor_tensor(lnd, lnd, gam.unsqueeze(1).to_broadcast([P, TB, D]), ALU.mult))
                step(eng.tensor_tensor(lnd, lnd, bet.unsqueeze(1).to_broadcast([P, TB, D]), ALU.add))
                step(eng.tensor_tensor(row, row, lnd, ALU.add))
                settled(eng)
                layernorm(eng, step, row, lnd, lnc, t4, b4[:, :])
                assert step.n == POST_STEPS
            with eng.Fori(0, DEPTH) as L:
                eng.wait_ge(tables_ready, L * 4 + 4)

                def step(j, G, Q, s, it=None):
                    g1, g2, g3 = (G - 1), (G - 2), (G - 3)
                    if active(s, 3):
                        eng.wait_ge(pv_done, g3 + 2)
                        eng.wait_ge(recip_done, g3 + 2)
                        eng.wait_ge(oT_done, g3 * 2 + 1)
                        for x in range(2):
                            dst = on[:, :].rearrange("p (m x h d) -> p x h m d", m=4, x=2, h=2)[:, x]
                            src = O(x).rearrange("p (h m d) -> p h m d", h=2, m=4)
                            r = rsum[:, :].rearrange("p (h m x) -> p x h m", h=2, x=2)[:, x].unsqueeze(3).to_broadcast([P, 2, 4, DH])
                            eng.tensor_tensor(dst, src, r, ALU.mult).then_inc(o_read, 1)
                    if active(s, 0):
                        r = j % 2
                        for i in range(2):
                            src = qk[:, i, :].rearrange("p (h d) -> p h d", d=DH)
                            if s is not None:
                                w = slice(DH * (s // 2), DH * (s // 2) + DH)
                            else:
                                w = bass.ds(it * (2 * DH) + DH * (j // 2), DH)
                            cos = tab[:, 2 * i, w].unsqueeze(1).to_broadcast([P, HEADS, DH])
                            sin = tab[:, 2 * i + 1, w].rearrange("p (u f) -> p u f", u=2).unsqueeze(1).to_broadcast([P, HEADS, 2, 32])
                            eng.wait_ge(r_evac, G * 6 + 2 + 2 * i + 1)
                            if s is None or s >= 2:
                                eng.wait_ge(qkT_done, g2 * 4 + 2 + 2 * i)
                            eng.tensor_tensor(cosp[:, r, i, :].rearrange("p (h d) -> p h d", d=DH), src, cos, ALU.mult).then_inc(rot_done, 1)
                            if s is None or s >= 1:
                                eng.wait_ge(rot_added, G * 2 - 1 + i + 1)
                            swapped = qk[:, i, :].rearrange("p (h u f) -> p h u f", u=2, f=32)[:, :, ::-1, :]
                            eng.tensor_tensor(sinp[:, i, :].rearrange("p (h u f) -> p h u f", u=2, f=32), swapped, sin, ALU.mult).then_inc(rot_done, 1)
                    if active(s, 3):
                        g = (j - 3) % 2
                        eng.wait_ge(y_done, g3 + 2)
                        if s is not None:
                            col = 1 + 32 * ((s - 3) // 2)
                            cols = slice(col, col + WIN)
                        else:
                            cols = bass.ds(it * (2 * WIN) + (1 + 32 * ((j - 3) // 2)), WIN)
                        eng.tensor_tensor(xb[:, GB * g:GB * g + GB, cols], R(7 * j + 6)[:, 0:P].rearrange("p (b t) -> p b t", b=GB),
                                          xa[:, GB * g:GB * g + GB, cols], ALU.add).then_inc(y_added, 1)
                    if active(s, 2):
                        eng.wait_ge(exp_done, g2 + 2)
                        eng.wait_ge(recip_done, g2 + 1)
                        eng.tensor_reduce(esum[:, :], ex[:, :].rearrange("p (h k) -> p h k", k=DH), AX_X, ALU.add).then_inc(rsum_done, 1)
                        eng.wait_ge(rsum_done, g2 + 2)
                        if active(s, 3):
                            eng.wait_ge(o_read, g3 * 2 + 3)
                        eng.reciprocal(rsum[:, :], esum[:, :]).then_inc(recip_done, 1)
                    if active(s, 0):
                        for i in range(2):
                            eng.wait_ge(sq_done, G * 2 + 1 + i + 1)
                            if i == 0:
                                eng.wait_ge(norm_step, G * (NSTEPS + 2) + 1)
                            eng.tensor_reduce(ssq[:, HEADS * i:HEADS * i + HEADS], sq[:, i, :].rearrange("p (h d) -> p h d", d=DH),
                                              AX_X, ALU.add).then_inc(ssq_done, 1)
                        base = G * (NSTEPS + 2)
                        eng.wait_ge(ssq_done, G * 2 + 3)
                        eng.tensor_scalar(ssq[:, :], ssq[:, :], 1e-24, None, ALU.max).then_inc(norm_step, 1)
                        eng.wait_ge(norm_step, base + 2)
                        rsqrt(eng, ssq[:, :], rbits[:, :], rhalf[:, :], rtmp[:, :], norm_step, base + 2)
                        eng.wait_ge(norm_step, base + 1 + NSTEPS + 1)
                        if s is None or s >= 1:
                            eng.wait_ge(rot_ready, G * 2 + 1)
                        eng.tensor_copy(rnorm[:, :], rtmp[:, :]).then_inc(norm_step, 1)
                    if active(s, 1):
                        eng.wait_ge(sims_done, g1 + 2)
                        eng.wait_ge(centered, g1 + 1)
                        eng.tensor_reduce(mx[:, :], scores, AX_X, ALU.max).then_inc(max_done, 1)
                        eng.wait_ge(max_done, g1 + 1)
                        eng.wait_ge(exp_done, g1 + 1)
                        eng.tensor_tensor(sh[:, :].rearrange("p (h k) -> p h k", k=DH), scores,
                                          mx[:, :].unsqueeze(2).to_broadcast([P, HEADS, DH]), ALU.subtract).then_inc(centered, 1)

                attention_steps(eng, L, step)
                eng.wait_ge(ffn_in, L * (16 * 13) + 16 * 13)

                def ffn(C, has_a, has_b, has_c, col=None):
                    c1, c2 = C - 1, C - 2
                    if has_c:
                        eng.wait_ge(fy_done, c2 + 2)
                        eng.scalar_tensor_tensor(out=xa[:, :, bass.ds(col, FW)], in0=ps[:, 6, :].rearrange("p (b t) -> p b t", b=BATCH),
                                                 scalar=vec[:, 2:3], in1=xb[:, :, bass.ds(col, FW)], op0=ALU.add, op1=ALU.add).then_inc(x_updated, 1)
                    if has_a:
                        eng.wait_ge(mean_done, C + 1)
                        eng.tensor_tensor(cc, xc, ps[:, 0, :], ALU.subtract).then_inc(ctr_done, 1)

                    def glu(m):
                        fn = FT[m][1]
                        eng.wait_ge(gelu_done, c1 * 3 + m + 1)
                        if m == 0:
                            eng.wait_ge(fy_done, c1 + 1)
                        eng.scalar_tensor_tensor(out=hh[0:fn, m, :], in0=ps[0:fn, 2 + 2 * (m % 2), :], scalar=vec[0:fn, 3 + m:4 + m],
                                                 in1=ge[0:fn, m, :], op0=ALU.add, op1=ALU.mult).then_inc(glu_done, 1)

                    if has_b:
                        glu(0)
                    if has_a:
                        base = C * (NSTEPS + 2) + 1
                        eng.wait_ge(var_done, C + 1)
                        eng.tensor_scalar(fx[:, :], ps[:, 7, 0:CH // P], EPS, None, ALU.add).then_inc(fnorm_step, 1)
                        eng.wait_ge(fnorm_step, base + 1)
                        rsqrt(eng, fx[:, :], fbits[:, :], fhalf[:, :], fr[:, :], fnorm_step, base + 1)
                        eng.wait_ge(fnorm_step, base + 1 + NSTEPS)
                        eng.tensor_tensor(dg.rearrange("p (g n) -> p g n", n=P), ident[:, :].unsqueeze(1).to_broadcast([P, CH // P, P]),
                                          fr[:, :].unsqueeze(2).to_broadcast([P, CH // P, P]), ALU.mult).then_inc(fnorm_step, 1)
                    if has_b:
                        glu(1)
                        glu(2)
                    if has_a:
                        eng.wait_ge(bc_done, C + 2)
                        eng.wait_ge(ctr_done, C + 2)
                        eng.wait_ge(affine_done, C + 1)
                        eng.tensor_tensor(xn, cc, ps[:, 1, :], ALU.mult).then_inc(xn_done, 1)

                ffn(L * NC, True, False, False)
                ffn(L * NC + 1, True, True, False)
                with eng.Fori(2, NC) as c:
                    ffn(eng.snap(L * NC + c), True, True, True, c * FW - (2 * FW - 1))
                ffn(L * NC + NC, False, True, True, (NC - 2) * FW + 1)
                ffn(L * NC + NC + 1, False, False, True, (NC - 1) * FW + 1)
            for b in range(BATCH):
                eng.wait_ge(x_updated, DEPTH * NC + 1)
                eng.wait_ge(end_turned, b + 1)
                eng.tensor_copy(hs.rearrange("p a n -> p (a n)"), xa[:, b, 1:1 + SEQ]).then_inc(end_read, 1)
                eng.wait_ge(end_turned, b + 2)
                if b >= 2:
                    eng.wait_ge((out_done2 if b % 2 else out_done), 16 * (b // 2))
                eng.tensor_tensor(fin[:, b % 2, :, :], ps[:, 0, :].rearrange("p (j d) -> p j d", j=TB), x1[:, b, :, :], ALU.add).then_inc(end_added, 1)


def rotary_tables():
    half = np.arange(0, DH, 2, dtype=np.float32)
    inv = (np.float32(1.0) / np.float32(10000.0) ** (half / np.float32(DH))).astype(np.float32)
    t = np.arange(SEQ, dtype=np.float32)
    f = t[:, None] * inv[None, :]
    f = np.concatenate([f, f], -1)
    base = (half + np.float32(0.4 * DH)) / np.float32(1.4 * DH)
    power = (t - SEQ // 2) / np.float32(WIN // 2)
    sc = (base[None, :] ** power[:, None]).astype(np.float32)
    sc = np.concatenate([sc, sc], -1)
    sign = np.where(np.arange(DH) < DH // 2, -1.0, 1.0).astype(np.float32)
    c, s = np.cos(f), np.sin(f) * sign
    inv_sc = np.float32(1.0) / sc
    full = np.stack([c * sc, s * sc, c * inv_sc, s * inv_sc]).astype(np.float32)
    tile = full.reshape(4, NW, WIN, DH).transpose(2, 0, 1, 3).reshape(WIN, 4, NW * DH)
    return np.ascontiguousarray(np.tile(tile, (GB, 1, 1)))


def mask_table():
    q = np.arange(WIN)[:, None]
    k = np.arange(WIN)[None, :]
    own = np.where(k <= q, 0.0, MASKED)
    before = np.where(k >= q, 0.0, MASKED)
    none = np.full((WIN, WIN), MASKED)
    m = np.stack([np.concatenate(x, 1) for x in ((own, before), (before, own), (own, none))], 1)
    return np.ascontiguousarray(np.tile(m, (GB, 1, 1)).astype(np.float32))


_INS = ["L0_attn_x", "L0_attn_A", "L0_attn_B", "L0_attn_C", "L0_attn_gamma", "L0_attn_beta", "L0_ffn_Wqkv", "L0_ffn_q_scale",
        "L0_ffn_k_scale", "L0_ffn_Wo", "L0_ffn_ln_g", "L0_ffn_ln_b", "L0_ffn_W1", "L0_ffn_b1", "L0_ffn_W2", "L0_ffn_b2"]


def kernel(**inputs):
    import concourse.bacc as bacc
    from concourse.bass_utils import run_bass_kernel_spmd

    nc = bacc.Bacc("TRN2", target_bir_lowering=False, num_devices=1)
    arrays, aps = {}, {}
    data = {n: np.ascontiguousarray(inputs[n]) for n in _INS}
    data.update(tab=rotary_tables(), mask=mask_table(), ident=np.eye(P, dtype=np.float32))
    for name, v in data.items():
        arrays["in_" + name] = v
        aps[name] = nc.dram_tensor("in_" + name, v.shape, mybir.dt.from_np(v.dtype), kind="ExternalInput").ap()
    aps["out"] = nc.dram_tensor("out_0", (BATCH, SEQ, D), F32, kind="ExternalOutput").ap()
    build(nc, aps)
    r = run_bass_kernel_spmd(nc, [arrays], core_ids=[0])
    return r.results[0]["out_0"]
```

```python
from contextlib import ExitStack

import numpy as np

import concourse.bass as bass
from concourse import mybir

ALU = mybir.AluOpType
ACT = mybir.ActivationFunctionType
AX_X = mybir.AxisListType.X
F32 = mybir.dt.float32
BF16 = mybir.dt.bfloat16
I32 = mybir.dt.int32

P = 128
BATCH, SEQ, D = 8, 512, 128
DEPTH, HEADS, DH, WIN = 6, 16, 64, 32
INNER = HEADS * DH
FF = int(D * 4 * 2 / 3)
FT = [(0, 128), (128, 128), (256, FF - 256)]
NW = SEQ // WIN
FW = 64
NC = SEQ // FW
LOG_NC = NC.bit_length() - 1
assert NC == 1 << LOG_NC and FW == 2 * WIN
CH = BATCH * FW
GB = P // WIN
NG = BATCH // GB
TILES = NW * NG
HP = HEADS // 2
ROUND = 4
TB = CH // P
EPS = 1e-5
MASKED = -1e30
MAGIC = 0x5F3759DF
NEWTON = 3
NSTEPS = 2 + 3 * NEWTON
SCALE = 8.0
TURNS = DEPTH * NC
NT = TURNS * ROUND


def rsqrt(eng, x, bits, half, y, sem, base):
    eng.tensor_scalar(bits, x.bitcast(I32), 1, None, ALU.logical_shift_right).then_inc(sem, 1)
    eng.wait_ge(sem, base + 1)
    eng.tensor_scalar(y.bitcast(I32), bits, -1, MAGIC, ALU.mult, ALU.add).then_inc(sem, 1)
    n = 2
    for _ in range(NEWTON):
        eng.wait_ge(sem, base + n)
        eng.tensor_tensor(half, y, y, ALU.mult).then_inc(sem, 1)
        eng.wait_ge(sem, base + n + 1)
        eng.scalar_tensor_tensor(out=half, in0=half, scalar=-0.5, in1=x, op0=ALU.mult, op1=ALU.mult).then_inc(sem, 1)
        eng.wait_ge(sem, base + n + 2)
        eng.scalar_tensor_tensor(out=y, in0=half, scalar=1.5, in1=y, op0=ALU.add, op1=ALU.mult).then_inc(sem, 1)
        n += 3


class Steps:

    def __init__(self, eng, sem, base):
        self.eng, self.sem, self.base, self.n = eng, sem, base, 0

    def __call__(self, ins):
        ins.then_inc(self.sem, 1)
        self.n += 1
        self.eng.wait_ge(self.sem, self.base + self.n)


def layernorm(eng, step, src, dst, c, t4, bits):
    shape = [P, TB, D]
    mean, var, half, r = (t4[:, i, :] for i in range(4))
    step(eng.tensor_reduce(mean, src, AX_X, ALU.add))
    step(eng.tensor_scalar(mean, mean, 1.0 / D, None, ALU.mult))
    step(eng.tensor_tensor(dst, src, mean.unsqueeze(2).to_broadcast(shape), ALU.subtract))
    step(eng.tensor_tensor(c, dst, dst, ALU.mult))
    step(eng.tensor_reduce(var, c, AX_X, ALU.add))
    step(eng.tensor_scalar(var, var, 1.0 / D, EPS, ALU.mult, ALU.add))
    rsqrt(eng, var, bits, half, r, step.sem, step.base + step.n)
    step.n += NSTEPS
    eng.wait_ge(step.sem, step.base + step.n)
    step(eng.tensor_tensor(dst, dst, r.unsqueeze(2).to_broadcast(shape), ALU.mult))


LN_STEPS = 7 + NSTEPS
POST_STEPS = 1 + LN_STEPS + 3 + LN_STEPS
O_EARLY = 3
KEEP = 512
AT_OUTPUT, AT_INPUT, AT_XN = 3, 38, 54
DMA_V = 2 * GB
DMA_W1 = 1 + 2 + 2 * len(FT)
DMA_W2 = len(FT) + 1


def build(nc, a):
    with ExitStack() as ctx:
        def sb(name, shape, dt=F32):
            return ctx.enter_context(nc.sbuf_tensor(name, shape, dt))

        def sem(name):
            return ctx.enter_context(nc.semaphore(name))

        ident = sb("ident", [P, P])
        ident_bf = sb("ident_bf", [P, P], BF16)
        ones = sb("ones", [P, P])
        mean_w = sb("mean_w", [P, P])
        mask = sb("mask", [P, NW * DH], BF16)
        x1 = sb("x1", [P, NC, TB, D])
        xa = sb("xa", [P, BATCH, 1 + SEQ])
        xb = sb("xb", [P, BATCH, 1 + SEQ])
        w_qkv = sb("w_qkv", [P, 3, INNER])
        w_o = sb("w_o", [P, HP, D])
        w_1 = sb("w_1", [P, 2 * FF])
        w_2 = sb("w_2", [P, 3, D])
        tab = sb("tab", [P, 2, 4, DH])
        qks = sb("qks", [P, 2, 4, DH])
        vec = sb("vec", [P, 9])
        xs = sb("xs", [P, 2, P])
        qk = sb("qk", [P, 2, INNER])
        cosp = sb("cosp", [P, 2, 2, INNER])
        sinp = sb("sinp", [P, 2, INNER])
        sq = sb("sq", [P, 2, INNER])
        ssq = sb("ssq", [P, 2 * HEADS])
        rbits = sb("rbits", [P, 2 * HEADS], I32)
        rhalf = sb("rhalf", [P, 2 * HEADS])
        rtmp = sb("rtmp", [P, 2 * HEADS])
        rnorm = sb("rnorm", [P, 2 * HEADS])
        qT = sb("qT", [P, HP, P])
        kT = sb("kT", [P, NG, HP, GB, 2 * WIN])
        sh = sb("sh", [P, INNER])
        ex = sb("ex", [P, INNER])
        mx = sb("mx", [P, HEADS])
        esum = sb("esum", [P, HEADS])
        rsum = sb("rsum", [P, HEADS])
        aT = sb("aT", [P, 8, P])
        vt = sb("vt", [P, 2, 2, 512])
        vk = sb("vk", [P, NG, GB, 512])
        on = sb("on", [P, INNER])
        oT = sb("oT", [P, HP, P])
        mask_f = ex
        rows = sb("rows", [P, 6, CH])
        xc, cc, cq, xn, xf, dg = (rows[:, i, :] for i in range(6))
        hh = sb("hh", [P, 3, CH])
        ge = sb("ge", [P, 3, CH])
        fx = sb("fx", [P, CH // P])
        fbits = sb("fbits", [P, CH // P], I32)
        fhalf = sb("fhalf", [P, CH // P])
        fr = sb("fr", [P, CH // P])
        xn_tm = cosp.rearrange("p a c n -> p (a c n)")[:, 0:2 * CH].rearrange("p (r j d) -> p r j d", r=2, j=TB)
        xn_fm = cosp.rearrange("p a c n -> p (a c n)")[:, 2 * CH:4 * CH].rearrange("p (r n) -> p r n", r=2)
        hb = qk.rearrange("p a n -> p (a n)")[:, 0:2 * CH].rearrange("p (r t b) -> p r t b", r=2, b=BATCH)
        lnc = sq.rearrange("p a n -> p (a n)")[:, 0:512].rearrange("p (j d) -> p j d", j=TB)
        lnd = sinp.rearrange("p a n -> p (a n)")[:, 0:512].rearrange("p (j d) -> p j d", j=TB)
        lno = on[:, 0:512].rearrange("p (j d) -> p j d", j=TB)
        hs = oT.rearrange("p (r j) n -> p r (j n)", r=2)
        abc = qT[:, 0:3, :]
        abcT = qT[:, 3:6, :]
        gam = aT[:, 0, :]
        bet = aT[:, 1, :]
        t4 = sb("t4", [P, 4, TB])
        b4 = sb("b4", [P, TB], I32)
        fin = cosp[:, 0, 0, :].rearrange("p (r j d) -> p r j d", r=2, j=TB)
        ps = ctx.enter_context(nc.psum_tensor("ps", [P, 8, 512], F32))

        consts_in = sem("consts_in")
        x_in = [sem(f"x_in{c}") for c in range(NC)]
        zeroed = sem("zeroed")
        abc_in = sem("abc_in")
        abc_turned = sem("abc_turned")
        abc_out = sem("abc_out")
        ln1_step = sem("ln1_step")
        ln1_turned = sem("ln1_turned")
        xn_out = sem("xn_out")
        pre_started = sem("pre_started")
        pre_done = sem("pre_done")
        h_done = sem("h_done")
        hs_done = sem("hs_done")
        post_step = sem("post_step")
        hs_turned = sem("hs_turned")
        post_turned = sem("post_turned")
        qkv_in = [sem(f"qkv_in{i}") for i in range(3)]
        tab_in = [sem(f"tab_in{i}") for i in range(2)]
        tab_ready = [sem(f"tab_ready{i}") for i in range(2)]
        wo_in = sem("wo_in")
        w1_in = sem("w1_in")
        w2_in = sem("w2_in")
        xs_ready = sem("xs_ready")
        proj_done = sem("proj_done")
        r_evac = sem("r_evac")
        rot_done = sem("rot_done")
        sq_done = sem("sq_done")
        ssq_done = sem("ssq_done")
        norm_step = sem("norm_step")
        rot_added = sem("rot_added")
        rot_ready = sem("rot_ready")
        qkT_done = sem("qkT_done")
        qk_evac = sem("qk_evac")
        sims_done = sem("sims_done")
        masked = sem("masked")
        max_done = sem("max_done")
        centered = sem("centered")
        exp_done = sem("exp_done")
        rsum_done = sem("rsum_done")
        recip_done = sem("recip_done")
        aT_done = sem("aT_done")
        at_evac = sem("at_evac")
        pv_done = sem("pv_done")
        o_read = sem("o_read")
        oT_done = sem("oT_done")
        ot_evac = sem("ot_evac")
        y_done = sem("y_done")
        y_added = sem("y_added")
        xc_ready = sem("xc_ready")
        mean_done = sem("mean_done")
        ctr_done = sem("ctr_done")
        csq_done = sem("csq_done")
        var_done = sem("var_done")
        fnorm_step = sem("fnorm_step")
        bc_done = sem("bc_done")
        xn_done = sem("xn_done")
        affine_done = sem("affine_done")
        hg_done = sem("hg_done")
        gate_out = sem("gate_out")
        a_out = sem("a_out")
        gelu_done = sem("gelu_done")
        glu_done = sem("glu_done")
        fy_done = sem("fy_done")
        x_updated = sem("x_updated")
        end_read = sem("end_read")
        end_turned = sem("end_turned")
        end_added = sem("end_added")
        out_done = [sem(f"out_done{i}") for i in range(2)]
        mask_in = sem("mask_in")

        from_one = (
            r_evac, proj_done, rot_done, y_done, y_added, ssq_done, sq_done, norm_step, sims_done, masked, centered,
            exp_done, rsum_done, recip_done, aT_done, pv_done, o_read, oT_done, glu_done, gate_out, a_out,
            xn_done, ctr_done, fy_done, fnorm_step, bc_done, affine_done, h_done, hs_done, hs_turned, ln1_step,
            post_step, xn_out, post_turned, pre_started, ln1_turned, end_added, end_turned, end_read, at_evac,
            rot_added, rot_ready, qk_evac, ot_evac,
        )

        def settled(eng):
            eng.sem_inc(carried[eng.engine.name], 1)

        carried = {n: sem("carried_" + n) for n in ("PE", "DVE", "Activation", "Pool", "SP")}
        v_landed = [sem(f"v_landed{i}") for i in range(ROUND)]
        block = ctx.enter_context(nc.Block())

        R = lambda n: ps[:, n % 2, :]
        T_ = lambda n: ps[:, 2 + n % 2, :]
        scores = ps[:, 4:6, :].rearrange("p a (h k) -> p (a h) k", k=DH)
        O = lambda x: ps[:, 6 + x, :]

        def pipeline(eng, step):
            for s in range(2 * ROUND):
                step(s % ROUND, s // ROUND, s)
            with eng.Fori(2, TURNS) as it:
                T = eng.snap(it)
                for j in range(ROUND):
                    step(j, T, None)
            for s in range(NT, NT + 2 * ROUND):
                step(s % ROUND, s // ROUND, s)

        def recurrence(eng, run):
            run(0, 0, True, False)
            with eng.Fori(0, (NC - 2) // 2) as it:
                run(eng.snap(it * 2 + 1), 1, False, False)
                run(eng.snap(it * 2 + 2), 0, False, False)
            run(NC - 1, (NC - 1) % 2, False, True)

        def active(s, back):
            return s is None or 0 <= s - back < NT

        def chunk(j, T, s):
            if s is None:
                return T - (1 if j == ROUND - 1 else 2)
            C = T - 1 if j == ROUND - 1 else T - 2
            return C if 0 <= C < TURNS else None

        def ended(j, T, s):
            C = T - 2
            return C if j == ROUND - 1 and (s is None or 0 <= C < TURNS) else None

        def leaving(s):
            n = -1 if s is None else s - NT - 3
            return range(2 * n, min(2 * n + 2, NC - 1)) if n >= 0 else ()

        def columns(eng, T, off, n):
            col = T % NC * FW if isinstance(T, int) else eng.snap((T & (NC - 1)) * FW)
            return slice(col + off, col + off + n) if isinstance(T, int) else bass.ds(col + off, n)

        @block.sync
        def _(eng):
            for name, dst in (("ident", ident[:, :]), ("mask", mask_f[:, :])):
                eng.dma_start(dst, a[name]).then_inc(consts_in, 16)
            for i, name in enumerate("ABC"):
                eng.dma_start(abc[:, i, :], a["L0_attn_" + name]).then_inc(abc_in, 16)
            for name, dst in (("L0_attn_gamma", gam), ("L0_attn_beta", bet)):
                eng.dma_start(dst, a[name].rearrange("(o d) -> o d", o=1).to_broadcast([P, D])).then_inc(abc_in, 16)
            for c in range(NC):
                for r in range(2):
                    eng.dma_start(x1[FW * r:FW * r + FW, c, :, :],
                                  a["L0_attn_x"].rearrange("(g r) (c t) d -> r c t g d", r=2, t=FW)[r, c]).then_inc(x_in[c], 16)
            for signal in from_one:
                eng.sem_inc(signal, 1)

            def load_table(w, T):
                known = isinstance(T, int)
                pos = bass.ds(T % NC * 2 + w if known else eng.snap((T & (NC - 1)) * 2 + w), 1)
                lay = bass.ds(T // NC if known else eng.snap(T >> LOG_NC), 1)
                eng.dma_start(tab[:, w, :, :].rearrange("p i d -> p (i d)"), a["tab"][pos, :, :].rearrange("o p n -> (o p) n")).then_inc(tab_in[w], 16)
                eng.dma_start(qks[:, w, :, :].rearrange("p i d -> p (i d)"), a["scales"][lay, :].to_broadcast([P, 4 * DH])).then_inc(tab_in[w], 16)

            def move_values(j, G):
                g, slot = j % 2, j // 2
                eng.wait_ge(r_evac, G * 6 + 7)
                settled(eng)
                if not isinstance(G, int) or G >= 2:
                    eng.wait_ge(pv_done, G)
                for x in range(2):
                    for b in range(GB):
                        eng.dma_start(vk[64 * x + 32 * slot:64 * x + 32 * slot + 32, g, b, :],
                                      vt[32 * b:32 * b + 32, j % 2, x, :]).then_inc(v_landed[j], 16)

            def turn(T, L=None, part=None):
                G = T * ROUND if isinstance(T, int) else eng.snap(T * ROUND)
                for j in range(ROUND):
                    if j or not isinstance(T, int) or T:
                        move_values((j - 1) % ROUND, G + (j - 1))
                    if j == 0:
                        eng.wait_ge(rot_done, G * 4 + 1)
                        settled(eng)
                        load_table(1, T)
                    if j == 2:
                        eng.wait_ge(rot_done, G * 4 + (4 * 2 + 1))
                        settled(eng)
                        load_table(0, T + 1)
                    if j == 2 and part == "wo":
                        eng.wait_ge(y_done, L * TILES + 1)
                        eng.dma_start(w_o[:, :, :], a["L0_ffn_Wo"][bass.ds(L, 1), :, :].rearrange("o (k p) n -> p (o k) n", p=P)).then_inc(wo_in, 16)
                    if j == 2 and part == "ffn":
                        eng.wait_ge(a_out, L * (3 * NC) + 1)
                        eng.wait_ge(gate_out, L * (3 * NC) + 1)
                        eng.dma_start(w_1[:, :], a["L0_ffn_W1"][bass.ds(L, 1), :, :].rearrange("o p n -> (o p) n")).then_inc(w1_in, 16)
                        for i, name in enumerate(("ln_g", "ln_b")):
                            eng.dma_start(vec[:, i:i + 1], a["L0_ffn_" + name][bass.ds(L, 1), :].rearrange("o p -> p o")).then_inc(w1_in, 16)
                        for u in range(2):
                            for m, (f0, fn) in enumerate(FT):
                                eng.dma_start(vec[0:fn, 3 + 3 * u + m:4 + 3 * u + m],
                                              a["L0_ffn_b1"][bass.ds(L, 1), u * FF + f0:u * FF + f0 + fn].rearrange("o p -> p o")).then_inc(w1_in, 16)
                    if j == 3 and part == "ffn":
                        eng.wait_ge(x_updated, L * NC + NC)
                        for m, (f0, fn) in enumerate(FT):
                            eng.dma_start(w_2[0:fn, m, :], a["L0_ffn_W2"][bass.ds(L, 1), f0:f0 + fn, :].rearrange("o p n -> (o p) n")).then_inc(w2_in, 16)
                        eng.dma_start(vec[:, 2:3], a["L0_ffn_b2"][bass.ds(L, 1), :].rearrange("o p -> p o")).then_inc(w2_in, 16)

            def layer(L, first=False):
                eng.wait_ge(proj_done, L * (6 * TILES) + 1)
                for c in range(3):
                    eng.dma_start(w_qkv[:, c, :], a["L0_ffn_Wqkv"][bass.ds(L, 1), :, INNER * c:INNER * c + INNER].rearrange("o p n -> (o p) n")).then_inc(qkv_in[c], 16)
                T0 = L * NC if first else eng.snap(L * NC)
                turn(T0, L, "wo")
                turn(T0 + 1 if first else eng.snap(T0 + 1), L, "ffn")
                with eng.Fori(2, NC) as it:
                    turn(eng.snap(T0 + it))

            load_table(0, 0)
            layer(0, True)
            with eng.Fori(1, DEPTH) as L:
                layer(L)
            move_values(ROUND - 1, NT - 1)
            for c in range(NC):
                eng.wait_ge(end_added, c + 2)
                for r in range(2):
                    eng.dma_start(a["out"].rearrange("(g r) (c t) d -> r c t g d", r=2, t=FW)[r, c],
                                  fin[FW * r:FW * r + FW, c % 2, :, :]).then_inc(out_done[c % 2], 16)
            eng.wait_ge(out_done[0], 16 * NC)
            eng.wait_ge(out_done[1], 16 * NC)

        @block.gpsimd
        def _(eng):
            eng.memset(ones[:, :], 1.0).then_inc(zeroed, 1)
            eng.memset(mean_w[:, :], 1.0 / D).then_inc(zeroed, 1)
            eng.memset(xa[:, :, 0:1], 0.0).then_inc(zeroed, 1)
            eng.memset(xb[:, :, 0:1], 0.0).then_inc(zeroed, 1)
            eng.memset(hb[:, 1, FW - 1, :], 0.0).then_inc(zeroed, 1)
            eng.memset(hh[:, :, :], 0.0).then_inc(zeroed, 1)
            eng.memset(ge[:, :, :], 0.0).then_inc(zeroed, 1)
            eng.memset(kT[:, :, :, :, :], 0.0).then_inc(zeroed, 1)
            eng.memset(vk[:, :, :, :], 0.0).then_inc(zeroed, 1)

            def run(c, r, first, last):
                eng.wait_ge(h_done, c * FW + (FW + 1))
                eng.wait_ge(hs_turned, c + 1)
                settled(eng)
                eng.tensor_copy(hs[:, 0, :].rearrange("p (b t) -> p b t", b=BATCH), hb[:, r, :, :].rearrange("p t b -> p b t")).then_inc(hs_done, 1)

            recurrence(eng, run)

            def scale_table(w, n):
                eng.wait_ge(tab_in[w], n * 32)
                settled(eng)
                eng.tensor_tensor(tab[:, w, :, :], tab[:, w, :, :], qks[:, w, :, :], ALU.mult).then_inc(tab_ready[w], 1)

            scale_table(0, 1)

            def step(j, T, s):
                if active(s, 1):
                    r, g1 = (j - 1) % 2, T * ROUND + (j - 1)
                    for i in range(2):
                        eng.wait_ge(rot_done, g1 * 4 + 2 * i + 3)
                        eng.tensor_tensor(cosp[:, r, i, :], cosp[:, r, i, :], sinp[:, i, :], ALU.add).then_inc(rot_added, 1)
                    eng.wait_ge(norm_step, g1 * (NSTEPS + 2) + NSTEPS + 3)
                    for i in range(2):
                        eng.wait_ge(rot_added, g1 * 2 + i + 2)
                        v = cosp[:, r, i, :].rearrange("p (h d) -> p h d", d=DH)
                        eng.tensor_tensor(v, v, rnorm[:, HEADS * i:HEADS * i + HEADS].unsqueeze(2).to_broadcast([P, HEADS, DH]),
                                          ALU.mult).then_inc(rot_ready, 1)
                C = ended(j, T, s)
                if C is not None:
                    eng.wait_ge(gelu_done, C * 2 + 2)
                    eng.wait_ge(a_out, C * 3 + 4)
                    settled(eng)
                    eng.tensor_tensor(hh[:, :, :], hh[:, :, :], ge[:, :, :], ALU.mult).then_inc(glu_done, 1)
                if active(s, 0) and j == 1:
                    scale_table(1, T + 1)
                if active(s, 0) and j == 3:
                    scale_table(0, T + 2)

            pipeline(eng, step)

        @block.tensor
        def _(eng):
            eng.wait_ge(abc_in, 16 * 5)
            eng.wait_ge(consts_in, 32)
            for i in range(3):
                eng.transpose(ps[:, 0, 128 * i:128 * i + 128], abc[:, i, :], ident[:, :]).then_inc(abc_turned, 1)

            def turn_xn(c, r):
                eng.wait_ge(ln1_step, c * LN_STEPS + (LN_STEPS + 1))
                eng.wait_ge(xn_out, c + 1)
                for j in range(TB):
                    t = eng.transpose(ps[:, 3, P * j:P * j + P], xn_tm[:, r, j, :], ident[:, :])
                t.then_inc(ln1_turned, 1)

            def outputs(c):
                eng.wait_ge(hs_done, c + 2)
                eng.wait_ge(post_step, c * POST_STEPS + 1)
                for j in range(TB):
                    t = eng.matmul(ps[:, 4, P * j:P * j + P], hs[:, 0, P * j:P * j + P], abcT[:, 2, :], start=True, stop=True)
                t.then_inc(hs_turned, 1)

            def turn_input(c):
                eng.wait_ge(post_step, c * POST_STEPS + (POST_STEPS + 1))
                if not isinstance(c, int) or c:
                    eng.wait_ge(x_updated, c)
                for j in range(TB):
                    t = eng.transpose(ps[:, 5, P * j:P * j + P], lnd[:, j, :], ident[:, :])
                t.then_inc(post_turned, 1)

            def run(c, r, first, last):
                eng.wait_ge(h_done, c * FW + 1)
                eng.wait_ge(xn_out, c + 2)
                settled(eng)
                eng.matmul(ps[:, r, :], abcT[:, 1, :], xn_fm[:, r, :].rearrange("p (b t) -> p t b", b=BATCH),
                           start=True, stop=False, skip_group_check=True).then_inc(pre_started, 1)
                for t in range(FW):
                    if t:
                        eng.wait_ge(h_done, c * FW + (t + 1))
                    prev = hb[:, r, t - 1, :] if t else hb[:, 1 - r, FW - 1, :]
                    eng.matmul(ps[:, r, BATCH * t:BATCH * t + BATCH], abcT[:, 0, :], prev, start=False, stop=t == FW - 1,
                               skip_group_check=True).then_inc(pre_done, 1)
                    for _ in range(2):
                        eng.matmul(ps[:, 7, 0:KEEP].rearrange("p (a n) -> p a n", n=P), ident_bf[:, :], ident_bf[:, :].unsqueeze(1).to_broadcast([P, KEEP // P, P]), start=True, stop=True)
                    if t == AT_OUTPUT and not first:
                        outputs(c - 1)
                    if t == AT_INPUT and not first:
                        turn_input(c - 1)
                    if t == AT_XN and not last:
                        turn_xn(c + 1, 1 - r)

            turn_xn(0, 0)
            eng.wait_ge(abc_out, 1)
            eng.wait_ge(zeroed, 9)
            eng.wait_ge(mask_in, 2)
            recurrence(eng, run)
            outputs(NC - 1)
            turn_input(NC - 1)

            def result(c):
                eng.wait_ge(end_read, c + 2)
                eng.wait_ge(end_added, c if c >= 2 else 1)
                eng.wait_ge(y_added, NT + 1)
                for j in range(TB):
                    t = eng.transpose(ps[:, c % 2, P * j:P * j + P], hs[:, c % 2, P * j:P * j + P], ident[:, :])
                t.then_inc(end_turned, 1)

            def step(j, T, s):
                G = T * ROUND + j
                g1, g2, g3 = G - 1, G - 2, G - 3
                gg = (j - 1) % 2
                C = chunk(j, T, s)
                Ce = ended(j, T, s)

                def project(c):
                    if j == 0 and c % 2 == 0:
                        eng.wait_ge(qkv_in[c // 2], (T >> LOG_NC) * 16 + 16)
                        settled(eng)
                    if c == 0:
                        eng.wait_ge(xs_ready, G * 2 + 2)
                        eng.wait_ge(r_evac, G * 6 + 1)
                    if c == 1 and (s is None or s >= 4):
                        eng.wait_ge(y_added, G - 2)
                    if c >= 2:
                        eng.wait_ge(r_evac, G * 6 + c)
                    if c < 4:
                        w = w_qkv[:, c // 2, 512 * (c % 2):512 * (c % 2) + 512]
                    else:
                        w = w_qkv[:, 2, :].rearrange("p (m x h d) -> p x h m d", m=4, x=2, h=2)[:, c % 2]
                    eng.matmul(R(7 * j + c), xs[:, j % 2, :], w, start=True, stop=True).then_inc(proj_done, 1)

                def turn(src, last, signal):
                    for u in range(2):
                        last(u)
                        for k in range(4):
                            n = 512 * u + 128 * k
                            t = eng.transpose(T_(u)[:, 128 * k:128 * k + 128], src[:, n:n + 128], ident[:, :])
                        t.then_inc(signal, 1)

                def bank_of_q(u):
                    if active(s, 3):
                        eng.wait_ge(at_evac, g3 * 2 + 2 + u)
                    elif s == 2:
                        eng.wait_ge(qk_evac, g1 * 4 + u)

                def bank_of_o(u):
                    if active(s, 1):
                        eng.wait_ge(qk_evac, g1 * 4 + 2 + u)
                    else:
                        eng.wait_ge(at_evac, g3 * 2 + 2 + u)

                def bank_of_k(u):
                    if active(s, 3):
                        eng.wait_ge(ot_evac, g3 * 2 + 2 + u)
                    else:
                        eng.wait_ge(qk_evac, g1 * 4 + 2 + u)

                def bank_of_e(u):
                    if active(s, 1):
                        eng.wait_ge(qk_evac, g1 * 4 + 4 + u)
                    else:
                        eng.wait_ge(ot_evac, g3 * 2 + 2 + u)

                def project_o(k):
                    t = eng.matmul(R(7 * j + 6)[:, 0:P], w_o[:, k, :], oT[:, k, :], start=k == 0, stop=k == HP - 1)
                    if k == HP - 1:
                        t.then_inc(y_done, 1)

                def weigh(n):
                    for i in range(4 * n, 4 * n + 4):
                        x, k = i // 8, i % 8
                        for b in range(GB):
                            t = eng.matmul(ps[32 * b:32 * b + 32, 6 + x, DH * k:DH * k + DH], aT[64 * x:64 * x + 64, k, 32 * b:32 * b + 32],
                                           vk[64 * x:64 * x + 64, (j - 3) % 2, b, DH * k:DH * k + DH], start=True, stop=True)
                    if n == 3:
                        t.then_inc(pv_done, 1)

                def w1(m):
                    f0, fn = FT[m]
                    for u in (1, 0):
                        t = eng.matmul(O(u)[0:fn], w_1[:, u * FF + f0:u * FF + f0 + fn], xf, start=True, stop=True)
                    t.then_inc(hg_done, 1)

                if active(s, 0):
                    project(0)
                    project(1)
                if active(s, 3):
                    eng.wait_ge(at_evac, g3 * 2 + 3)
                    before = ((j - 1) % ROUND, T if j else T - 1, None if s is None else s - 1)
                    Cp, Cq = chunk(*before), ended(*before)
                    if Cp is not None and j == 0:
                        eng.wait_ge(fnorm_step, Cp * (NSTEPS + 2) + 2)
                    if Cp is not None and j == 1:
                        eng.wait_ge(xn_done, Cp + 2)
                    if Cp is not None and j in (2, 3):
                        eng.wait_ge(gate_out, Cp * 3 + j + 1)
                        eng.wait_ge(a_out, Cp * 3 + j + 1)
                    if Cq is not None:
                        eng.wait_ge(x_updated, Cq + NC + 1)
                    eng.wait_ge(o_read, g3 * 2 + 1)
                    eng.wait_ge(v_landed[(j - 3) % ROUND], (T + ((j - 3) // ROUND + 1)) * (16 * DMA_V))
                    settled(eng)
                for n in range(4):
                    if active(s, 3):
                        weigh(n)
                    if active(s, 0) and n < 3:
                        project(2 + n)
                if active(s, 1):
                    eng.wait_ge(rot_ready, g1 * 2 + 2)
                    turn(cosp[:, (j - 1) % 2, 0, :], bank_of_q, qkT_done)
                if active(s, 0):
                    project(5)
                if active(s, 3):
                    eng.wait_ge(o_read, g3 * 2 + 3)
                    turn(on, bank_of_o, oT_done)
                if C is not None and j == 3:
                    eng.wait_ge(xc_ready, C * 2 + 2)
                    if s is None or s > 2 * ROUND - 1:
                        eng.wait_ge(a_out, C * 3 + 1)
                    eng.matmul(O(0), mean_w[:, :], xc, start=True, stop=True).then_inc(mean_done, 1)
                if C is not None and j == 0:
                    eng.wait_ge(fnorm_step, C * (NSTEPS + 2) + NSTEPS + 3)
                    eng.matmul(O(0), ones[:, :], dg, start=True, stop=True).then_inc(bc_done, 1)
                if C is not None and j == 1:
                    eng.wait_ge(w1_in, (C >> LOG_NC) * (16 * DMA_W1) + 16 * DMA_W1)
                    settled(eng)
                    eng.wait_ge(affine_done, C + 2)
                    w1(0)
                if C is not None and j == 2:
                    eng.wait_ge(gate_out, C * 3 + 3)
                    eng.wait_ge(a_out, C * 3 + 3)
                    w1(2)
                if active(s, 1):
                    eng.wait_ge(rot_ready, g1 * 2 + 3)
                    turn(cosp[:, (j - 1) % 2, 1, :], bank_of_k, qkT_done)
                if active(s, 3):
                    if active(s, 0):
                        eng.wait_ge(r_evac, G * 6 + 6)
                    else:
                        eng.wait_ge(r_evac, 6 * NT + 1)
                        eng.wait_ge(y_added, g3 + 1)
                    if j == 3:
                        eng.wait_ge(wo_in, (T >> LOG_NC) * 16 + 16)
                        settled(eng)
                    eng.wait_ge(ot_evac, g3 * 2 + 3)
                    for k in range(O_EARLY):
                        project_o(k)
                if active(s, 2):
                    eng.wait_ge(exp_done, g2 + 2)
                    turn(ex, bank_of_e, aT_done)
                if C is not None and j == 1:
                    eng.wait_ge(gate_out, C * 3 + 2)
                    eng.wait_ge(a_out, C * 3 + 2)
                    w1(1)
                if Ce is not None:
                    eng.wait_ge(w2_in, (Ce >> LOG_NC) * (16 * DMA_W2) + 16 * DMA_W2)
                    settled(eng)
                    eng.wait_ge(glu_done, Ce + 2)
                    if C is not None:
                        eng.wait_ge(ctr_done, C + 2)
                    for m, (f0, fn) in enumerate(FT):
                        t = eng.matmul(O(0), w_2[0:fn, m, :], hh[0:fn, m, :], start=m == 0, stop=m == 2)
                    t.then_inc(fy_done, 1)
                if C is not None and j == 3:
                    eng.wait_ge(csq_done, C + 1)
                    for g in range(CH // P):
                        t = eng.matmul(ps[:, 7, g:g + 1], cq[:, P * g:P * g + P], mean_w[:, 0:1], start=True, stop=True)
                    t.then_inc(var_done, 1)
                if active(s, 1):
                    eng.wait_ge(masked, g1 + 1)
                    eng.wait_ge(qk_evac, g1 * 4 + 5)
                    settled(eng)
                for k in range(HP):
                    if active(s, 3) and O_EARLY + k < HP:
                        project_o(O_EARLY + k)
                    if active(s, 1):
                        h2 = k // 4
                        rows = slice(64 * h2, 64 * h2 + 64)
                        for hp in (2 * k % HP, 2 * k % HP + 1):
                            for b in range(GB):
                                t = eng.matmul(ps[32 * b:32 * b + 32, 4 + h2, DH * hp:DH * hp + DH], qT[rows, hp, 32 * b:32 * b + 32],
                                               kT[rows, gg, hp, b, :], start=True, stop=True)
                        if k == HP - 1:
                            t.then_inc(sims_done, 1)
                for c in leaving(s):
                    result(c)

            pipeline(eng, step)
            result(NC - 1)

        @block.scalar
        def _(eng):
            eng.wait_ge(abc_turned, 3)
            eng.copy(abcT.rearrange("p a n -> p (a n)"), ps[:, 0, 0:384]).then_inc(abc_out, 1)

            def take_xn(c, r):
                eng.wait_ge(ln1_turned, c + 2)
                if not isinstance(c, int) or c > 1:
                    eng.wait_ge(pre_started, c)
                eng.copy(xn_fm[:, r, :], ps[:, 3, :]).then_inc(xn_out, 1)

            def take_input(c):
                eng.wait_ge(post_turned, c + 2)
                settled(eng)
                eng.copy(xa[:, :, columns(eng, c, 1, FW)], ps[:, 5, :].rearrange("p (b t) -> p b t", b=BATCH)).then_inc(x_updated, 1)

            def run(c, r, first, last):
                for t in range(FW):
                    if t == 0:
                        eng.wait_ge(hs_done, c if not isinstance(c, int) or c else 1)
                    eng.wait_ge(pre_done, c * FW + (t + 1))
                    eng.activation(hb[:, r, t, :], ps[:, r, BATCH * t:BATCH * t + BATCH], ACT.Tanh).then_inc(h_done, 1)
                    if t == AT_INPUT and not first:
                        take_input(c - 1)
                    if t == AT_XN and not last:
                        take_xn(c + 1, 1 - r)

            take_xn(0, 0)
            recurrence(eng, run)
            take_input(NC - 1)

            def shifted(dst, src, batches, T, off, signal, n):
                for h in range(2):
                    rows = slice(64 * h, 64 * h + 64)
                    eng.copy(dst[rows], src[rows, batches, columns(eng, T, off + 1 - h, n)]).then_inc(signal, 1)

            def tile_input(j, T, s):
                G = T * ROUND + j
                if s is None or s >= 2:
                    eng.wait_ge(proj_done, G * 6 - 5)
                if j == 0:
                    eng.wait_ge(x_updated, T + 1)
                settled(eng)
                shifted(xs[:, j % 2, :].rearrange("p (b t) -> p b t", b=GB), xa, slice(GB * (j % 2), GB * (j % 2) + GB),
                        T, WIN * (j // 2), xs_ready, WIN)

            def result(c):
                eng.wait_ge(x_updated, DEPTH * NC + c + 1)
                eng.wait_ge(y_done, NT + 1)
                if c >= 2:
                    eng.wait_ge(end_turned, c)
                eng.copy(hs[:, c % 2, :].rearrange("p (b t) -> p b t", b=BATCH), xa[:, :, 1 + FW * c:1 + FW * c + FW]).then_inc(end_read, 1)

            def step(j, T, s):
                G = T * ROUND + j
                g1, g2, g3 = G - 1, G - 2, G - 3
                C = chunk(j, T, s)

                def take(c):
                    if c == 0:
                        eng.wait_ge(sq_done, G * 2 + 1)
                    if c in (0, 2) and (s is None or s >= 1):
                        eng.wait_ge(rot_done, G * 4 - 1 + c)
                    if c == 4 and (s is None or s >= 2):
                        eng.wait_ge(v_landed[(j - 2) % ROUND], (T + ((j - 2) // ROUND + 1)) * (16 * DMA_V))
                    eng.wait_ge(proj_done, G * 6 + c + 2)
                    dst = qk[:, c // 2, 512 * (c % 2):512 * (c % 2) + 512] if c < 4 else vt[:, j % 2, c % 2, :]
                    eng.copy(dst, R(7 * j + c)).then_inc(r_evac, 1)

                def gate(m):
                    fn = FT[m][1]
                    eng.wait_ge(hg_done, C * 3 + m + 1)
                    eng.activation(ge[0:fn, m, :], O(1)[0:fn], ACT.Identity, bias=vec[0:fn, 6 + m:7 + m]).then_inc(gate_out, 1)

                def square(i):
                    if i or s is None or s >= 1:
                        eng.wait_ge(ssq_done, G * 2 + i)
                    eng.wait_ge(r_evac, G * 6 + 3 + 2 * i)
                    eng.activation(sq[:, i, :], qk[:, i, :], ACT.Square).then_inc(sq_done, 1)

                if active(s, 0):
                    take(0)
                    take(1)
                    take(2)
                if active(s, 2):
                    eng.wait_ge(centered, g2 + 2)
                    eng.wait_ge(rsum_done, g2 + 1)
                    eng.wait_ge(aT_done, g2 * 2 + 1)
                    eng.activation(ex[:, :], sh[:, :], ACT.Exp, scale=SCALE).then_inc(exp_done, 1)
                if active(s, 0):
                    square(0)
                    take(3)
                    take(4)
                    square(1)
                if active(s, 1):
                    eng.wait_ge(sims_done, g1 + 1)
                    for u in range(2):
                        eng.wait_ge(qkT_done, g1 * 4 + 1 + u)
                        eng.copy(qT[:, 4 * u:4 * u + 4, :].rearrange("p a n -> p (a n)"), T_(u)).then_inc(qk_evac, 1)
                if active(s, 0):
                    take(5)
                if active(s, 3):
                    eng.wait_ge(y_done, g3 + 1)
                    for u in range(2):
                        eng.wait_ge(oT_done, g3 * 2 + 2 + u)
                        eng.copy(oT[:, 4 * u:4 * u + 4, :].rearrange("p a n -> p (a n)"), T_(u)).then_inc(ot_evac, 1)
                if active(s, 1):
                    gg, slot = (j - 1) % 2, ((j - 1) % ROUND) // 2
                    for u in range(2):
                        eng.wait_ge(qkT_done, g1 * 4 + 3 + u)
                        dst = kT[:, gg, 4 * u:4 * u + 4, :, 32 * slot:32 * slot + 32]
                        eng.copy(dst, T_(u).rearrange("p (h b t) -> p h b t", h=4, b=GB)).then_inc(qk_evac, 1)
                if C is not None and j == 3:
                    eng.wait_ge(ctr_done, C + 2)
                    eng.activation(cq, cc, ACT.Square).then_inc(csq_done, 1)
                if C is not None and j == 0:
                    eng.wait_ge(w1_in, (C >> LOG_NC) * (16 * DMA_W1) + 16 * DMA_W1)
                    settled(eng)
                    eng.wait_ge(xn_done, C + 2)
                    eng.activation(xf, xn, ACT.Identity, bias=vec[:, 1:2], scale=vec[:, 0:1]).then_inc(affine_done, 1)
                if C is not None and j in (1, 2):
                    gate(2 * (j - 1))
                if active(s, 2):
                    eng.wait_ge(pv_done, g2 + 1)
                    for u in range(2):
                        eng.wait_ge(aT_done, g2 * 2 + 2 + u)
                        eng.copy(aT[:, 4 * u:4 * u + 4, :].rearrange("p a n -> p (a n)"), T_(u)).then_inc(at_evac, 1)
                if s is None or s + 1 < NT:
                    tile_input((j + 1) % ROUND, T if j < ROUND - 1 else eng.snap(T + 1) if s is None else T + 1, None if s is None else s + 1)
                if C is not None and j == 1:
                    gate(1)
                if C is not None and j == 2:
                    eng.wait_ge(gate_out, C * 3 + 4)
                    settled(eng)
                    eng.activation(ge[:, 0:2, :], ge[:, 0:2, :], ACT.Gelu).then_inc(gelu_done, 1)
                    eng.activation(ge[0:FT[2][1], 2, :], ge[0:FT[2][1], 2, :], ACT.Gelu).then_inc(gelu_done, 1)
                if j == 2 and (s is None or 0 <= T - 1 < TURNS):
                    eng.wait_ge(y_added, T * ROUND + 1)
                    settled(eng)
                    shifted(xc.rearrange("p (b t) -> p b t", b=BATCH), xb, slice(0, BATCH), T - 1, 0, xc_ready, FW)
                for c in leaving(s):
                    result(c)

            tile_input(0, 0, 0)
            pipeline(eng, step)
            result(NC - 1)

        @block.vector
        def _(eng):
            eng.wait_ge(consts_in, 32)
            eng.tensor_copy(ident_bf[:, :], ident[:, :]).then_inc(mask_in, 1)
            eng.tensor_copy(mask[:, :], mask_f[:, :]).then_inc(mask_in, 1)

            def normalise(c, r):
                row = x1[:, c, :, :] if isinstance(c, int) else x1[:, bass.ds(c, 1), :, :].rearrange("p o j d -> p (o j) d")
                if not isinstance(c, int) or c > 1:
                    eng.wait_ge(ln1_turned, c)
                settled(eng)
                step = Steps(eng, ln1_step, c * LN_STEPS + 1)
                layernorm(eng, step, row, xn_tm[:, r, :, :], lnc, t4, b4[:, :])
                assert step.n == LN_STEPS

            def post(c, r):
                row = x1[:, c, :, :] if isinstance(c, int) else x1[:, bass.ds(c, 1), :, :].rearrange("p o j d -> p (o j) d")
                eng.wait_ge(hs_turned, c + 2)
                eng.wait_ge(post_turned, c + 1)
                settled(eng)
                step = Steps(eng, post_step, c * POST_STEPS + 1)
                step(eng.tensor_tensor(lno, ps[:, 4, :].rearrange("p (j d) -> p j d", j=TB), xn_tm[:, r, :, :], ALU.add))
                layernorm(eng, step, lno, lnd, lnc, t4, b4[:, :])
                step(eng.tensor_tensor(lnd, lnd, gam.unsqueeze(1).to_broadcast([P, TB, D]), ALU.mult))
                step(eng.tensor_tensor(lnd, lnd, bet.unsqueeze(1).to_broadcast([P, TB, D]), ALU.add))
                step(eng.tensor_tensor(row, row, lnd, ALU.add))
                settled(eng)
                layernorm(eng, step, row, lnd, lnc, t4, b4[:, :])
                assert step.n == POST_STEPS

            def run(c, r, first, last):
                if not first:
                    post(c - 1, 1 - r)
                if not last:
                    normalise(c + 1, 1 - r)

            eng.wait_ge(x_in[0], 32)
            normalise(0, 0)
            for c in range(1, NC):
                eng.wait_ge(x_in[c], 32)
            eng.wait_ge(abc_in, 16 * 5)
            recurrence(eng, run)
            post(NC - 1, (NC - 1) % 2)

            def result(c):
                eng.wait_ge(end_turned, c + 2)
                if c >= 2:
                    eng.wait_ge(out_done[c % 2], 32 * (c // 2))
                eng.tensor_tensor(fin[:, c % 2, :, :], ps[:, c % 2, :].rearrange("p (j d) -> p j d", j=TB), x1[:, c, :, :], ALU.add).then_inc(end_added, 1)

            def step(j, T, s):
                G = T * ROUND + j
                g1, g2, g3 = G - 1, G - 2, G - 3
                C = chunk(j, T, s)

                Ce = ended(j, T, s)

                def take_a(m):
                    fn = FT[m][1]
                    eng.wait_ge(hg_done, C * 3 + m + 1)
                    eng.tensor_scalar(hh[0:fn, m, :], O(0)[0:fn], vec[0:fn, 3 + m:4 + m], None, ALU.add).then_inc(a_out, 1)

                def normalise_o():
                    eng.wait_ge(pv_done, g3 + 2)
                    eng.wait_ge(recip_done, g3 + 2)
                    eng.wait_ge(oT_done, g3 * 2 + 1)
                    for x in range(2):
                        dst = on[:, :].rearrange("p (m x h d) -> p x h m d", m=4, x=2, h=2)[:, x]
                        src = O(x).rearrange("p (h m d) -> p h m d", h=2, m=4)
                        r = rsum[:, :].rearrange("p (h m x) -> p x h m", h=2, x=2)[:, x].unsqueeze(3).to_broadcast([P, 2, 4, DH])
                        eng.tensor_tensor(dst, src, r, ALU.mult).then_inc(o_read, 1)
                if active(s, 0):
                    r = j % 2
                    if j % 2 == 0:
                        eng.wait_ge(tab_ready[j // 2], T + 1)
                        settled(eng)
                    for i in range(2):
                        src = qk[:, i, :].rearrange("p (h d) -> p h d", d=DH)
                        cos = tab[:, j // 2, 2 * i, :].unsqueeze(1).to_broadcast([P, HEADS, DH])
                        sin = tab[:, j // 2, 2 * i + 1, :].rearrange("p (u f) -> p u f", u=2).unsqueeze(1).to_broadcast([P, HEADS, 2, 32])
                        eng.wait_ge(r_evac, G * 6 + 2 + 2 * i + 1)
                        if s is None or s >= 2:
                            eng.wait_ge(qkT_done, g2 * 4 + 2 + 2 * i)
                        eng.tensor_tensor(cosp[:, r, i, :].rearrange("p (h d) -> p h d", d=DH), src, cos, ALU.mult).then_inc(rot_done, 1)
                        if s is None or s >= 1:
                            eng.wait_ge(rot_added, G * 2 - 1 + i + 1)
                        swapped = qk[:, i, :].rearrange("p (h u f) -> p h u f", u=2, f=32)[:, :, ::-1, :]
                        eng.tensor_tensor(sinp[:, i, :].rearrange("p (h u f) -> p h u f", u=2, f=32), swapped, sin, ALU.mult).then_inc(rot_done, 1)
                        if i == 0 and active(s, 3):
                            normalise_o()
                elif active(s, 3):
                    normalise_o()
                if active(s, 2):
                    eng.wait_ge(exp_done, g2 + 2)
                    eng.wait_ge(recip_done, g2 + 1)
                    eng.tensor_reduce(esum[:, :], ex[:, :].rearrange("p (h k) -> p h k", k=DH), AX_X, ALU.add).then_inc(rsum_done, 1)
                    eng.wait_ge(rsum_done, g2 + 2)
                    if active(s, 3):
                        eng.wait_ge(o_read, g3 * 2 + 3)
                    eng.reciprocal(rsum[:, :], esum[:, :]).then_inc(recip_done, 1)
                if C is not None and j == 3:
                    eng.wait_ge(mean_done, C + 1)
                    eng.tensor_tensor(cc, xc, O(0), ALU.subtract).then_inc(ctr_done, 1)
                if C is not None and j == 0:
                    eng.wait_ge(bc_done, C + 2)
                    eng.tensor_tensor(xn, cc, O(0), ALU.mult).then_inc(xn_done, 1)
                if C is not None and j in (1, 2):
                    if j == 1:
                        eng.wait_ge(w1_in, (C >> LOG_NC) * (16 * DMA_W1) + 16 * DMA_W1)
                        settled(eng)
                    take_a(2 * (j - 1))
                if active(s, 0):
                    for i in range(2):
                        eng.wait_ge(sq_done, G * 2 + 1 + i + 1)
                        if i == 0:
                            eng.wait_ge(norm_step, G * (NSTEPS + 2) + 1)
                        eng.tensor_reduce(ssq[:, HEADS * i:HEADS * i + HEADS], sq[:, i, :].rearrange("p (h d) -> p h d", d=DH),
                                          AX_X, ALU.add).then_inc(ssq_done, 1)
                    base = G * (NSTEPS + 2)
                    eng.wait_ge(ssq_done, G * 2 + 3)
                    eng.tensor_scalar(ssq[:, :], ssq[:, :], 1e-24, None, ALU.max).then_inc(norm_step, 1)
                    eng.wait_ge(norm_step, base + 2)
                    rsqrt(eng, ssq[:, :], rbits[:, :], rhalf[:, :], rtmp[:, :], norm_step, base + 2)
                    eng.wait_ge(norm_step, base + 1 + NSTEPS + 1)
                    if s is None or s >= 1:
                        eng.wait_ge(rot_ready, G * 2 + 1)
                    eng.tensor_copy(rnorm[:, :], rtmp[:, :]).then_inc(norm_step, 1)
                if C is not None and j == 1:
                    take_a(1)
                if C is not None and j == 3:
                    eng.wait_ge(var_done, C + 1)
                    eng.tensor_scalar(fx[:, :], ps[:, 7, 0:CH // P], EPS, None, ALU.add).then_inc(fnorm_step, 1)
                if Ce is not None:
                    eng.wait_ge(w2_in, (Ce >> LOG_NC) * (16 * DMA_W2) + 16 * DMA_W2)
                    settled(eng)
                    eng.wait_ge(fy_done, Ce + 2)
                    cols = columns(eng, Ce, 1, FW)
                    eng.scalar_tensor_tensor(out=xa[:, :, cols], in0=O(0).rearrange("p (b t) -> p b t", b=BATCH),
                                             scalar=vec[:, 2:3], in1=xb[:, :, cols], op0=ALU.add, op1=ALU.add).then_inc(x_updated, 1)
                if active(s, 3):
                    g = (j - 3) % 2
                    eng.wait_ge(y_done, g3 + 2)
                    cols = columns(eng, T if j == 3 else T - 1, 1 + WIN * ((j - 3) % ROUND // 2), WIN)
                    eng.tensor_tensor(xb[:, GB * g:GB * g + GB, cols], R(7 * j + 6)[:, 0:P].rearrange("p (b t) -> p b t", b=GB),
                                      xa[:, GB * g:GB * g + GB, cols], ALU.add).then_inc(y_added, 1)
                if active(s, 1):
                    eng.wait_ge(sims_done, g1 + 2)
                    eng.wait_ge(exp_done, g1 + 1)
                    T1 = T if j else T - 1
                    at = DH * ((j - 1) % ROUND // 2)
                    if isinstance(T, int):
                        w = slice(2 * DH * (T1 % NC) + at, 2 * DH * (T1 % NC) + at + DH)
                    else:
                        settled(eng)
                        w = bass.ds(eng.snap((T1 & (NC - 1)) * (2 * DH)) + at, DH)
                    e = sh[:, :].rearrange("p (h k) -> p h k", k=DH)
                    eng.tensor_tensor(e, scores, mask[:, w].unsqueeze(1).to_broadcast([P, HEADS, DH]), ALU.add).then_inc(masked, 1)
                    eng.wait_ge(masked, g1 + 2)
                    eng.tensor_reduce(mx[:, :], e, AX_X, ALU.max).then_inc(max_done, 1)
                    eng.wait_ge(max_done, g1 + 1)
                    eng.tensor_tensor(e, e, mx[:, :].unsqueeze(2).to_broadcast([P, HEADS, DH]), ALU.subtract).then_inc(centered, 1)
                if C is not None and j == 3:
                    base = C * (NSTEPS + 2) + 1
                    eng.wait_ge(fnorm_step, base + 1)
                    rsqrt(eng, fx[:, :], fbits[:, :], fhalf[:, :], fr[:, :], fnorm_step, base + 1)
                    eng.wait_ge(fnorm_step, base + 1 + NSTEPS)
                    eng.tensor_tensor(dg.rearrange("p (g n) -> p g n", n=P), ident[:, :].unsqueeze(1).to_broadcast([P, CH // P, P]),
                                      fr[:, :].unsqueeze(2).to_broadcast([P, CH // P, P]), ALU.mult).then_inc(fnorm_step, 1)
                for c in leaving(s):
                    result(c)

            pipeline(eng, step)
            result(NC - 1)

def rotary_tables():
    half = np.arange(0, DH, 2, dtype=np.float32)
    inv = (np.float32(1.0) / np.float32(10000.0) ** (half / np.float32(DH))).astype(np.float32)
    t = np.arange(SEQ, dtype=np.float32)
    f = t[:, None] * inv[None, :]
    f = np.concatenate([f, f], -1)
    base = (half + np.float32(0.4 * DH)) / np.float32(1.4 * DH)
    power = (t - SEQ // 2) / np.float32(WIN // 2)
    sc = (base[None, :] ** power[:, None]).astype(np.float32)
    sc = np.concatenate([sc, sc], -1)
    sign = np.where(np.arange(DH) < DH // 2, -1.0, 1.0).astype(np.float32)
    c, s = np.cos(f), np.sin(f) * sign
    inv_sc = np.float32(1.0) / sc
    full = np.stack([c * sc, s * sc, c * inv_sc, s * inv_sc]).astype(np.float32)
    tile = full.reshape(4, NW, WIN, DH).transpose(1, 2, 0, 3).reshape(NW, WIN, 4 * DH)
    return np.ascontiguousarray(np.tile(tile, (1, GB, 1)))


def mask_table():
    q = np.arange(WIN)[:, None]
    k = np.arange(WIN)[None, :]
    own = np.where(k <= q, 0.0, MASKED)
    before = np.where(k >= q, 0.0, MASKED)
    none = np.full((WIN, WIN), MASKED)
    m = np.concatenate([np.concatenate((own, before if w else none) if w % 2 == 0 else (before, own), 1) for w in range(NW)], 1)
    return np.ascontiguousarray(np.tile(m, (GB, 1)).astype(np.float32))


def scale_rows(q, k):
    def swap(v):
        return np.concatenate((v[:, DH // 2:], v[:, :DH // 2]), 1)
    rows = np.concatenate((q, swap(q), k, swap(k)), 1)
    return np.ascontiguousarray(np.concatenate((rows, rows[-1:]), 0))


_INS = ["L0_attn_x", "L0_attn_A", "L0_attn_B", "L0_attn_C", "L0_attn_gamma", "L0_attn_beta", "L0_ffn_Wqkv",
        "L0_ffn_Wo", "L0_ffn_ln_g", "L0_ffn_ln_b", "L0_ffn_W1", "L0_ffn_b1", "L0_ffn_W2", "L0_ffn_b2"]


def kernel(**inputs):
    import concourse.bacc as bacc
    from concourse.bass_utils import run_bass_kernel_spmd

    nc = bacc.Bacc("TRN2", target_bir_lowering=False, num_devices=1)
    arrays, aps = {}, {}
    data = {n: np.ascontiguousarray(inputs[n]) for n in _INS}
    data.update(scales=scale_rows(np.asarray(inputs["L0_ffn_q_scale"]), np.asarray(inputs["L0_ffn_k_scale"])))
    data.update(tab=rotary_tables(), mask=mask_table(), ident=np.eye(P, dtype=np.float32))
    for name, v in data.items():
        arrays["in_" + name] = v
        aps[name] = nc.dram_tensor("in_" + name, v.shape, mybir.dt.from_np(v.dtype), kind="ExternalInput").ap()
    aps["out"] = nc.dram_tensor("out_0", (BATCH, SEQ, D), F32, kind="ExternalOutput").ap()
    build(nc, aps)
    r = run_bass_kernel_spmd(nc, [arrays], core_ids=[0])
    return r.results[0]["out_0"]
```
